# Optimizing a Trainium2 kernel written in Bass

```python
import numpy as np
import jax
import jax.numpy as jnp

def _softmax(x, axis=-1):
    return jax.nn.softmax(x, axis=axis)

def _gelu(x):
    return jax.nn.gelu(x, approximate=True)

def _silu(x):
    return jax.nn.silu(x)

def _sigmoid(x):
    return jax.nn.sigmoid(x)

def _layernorm(x, axis=-1, eps=1e-05):
    m = jnp.mean(x, axis=axis, keepdims=True)
    v = jnp.var(x, axis=axis, keepdims=True)
    return (x - m) / jnp.sqrt(v + eps)

def _scatter_add(tgt, idx, src, axis=0):
    return tgt.at[idx].add(src)

def _segment_sum(src, seg, n):
    return jax.ops.segment_sum(src, seg, n)
kernel_name = 'mk_gnn_resnorm_d2_gnn_r8_a07035'

def setup_inputs(seed: int=0):
    np.random.seed(seed)
    _w = jnp.asarray

    def _rec_inputs():
        import jax
        import jax.numpy as jnp
        _gk = jax.random.key(seed)
        x = -0.000202 + 1 * jax.random.normal(jax.random.fold_in(_gk, 1), (12500, 64), jnp.float32)
        _s = jax.random.randint(jax.random.fold_in(_gk, 2), (100000,), 0, 12500, jnp.int32)
        _d = jax.random.randint(jax.random.fold_in(_gk, 3), (100000,), 0, 12500, jnp.int32)
        _loop = jnp.arange(12500, dtype=jnp.int32)
        src = jnp.concatenate([_s, _d, _loop])
        dst = jnp.concatenate([_d, _s, _loop])
        _o = jnp.argsort(dst, stable=True)
        src = src[_o]
        dst = dst[_o]
        edge_attr_64 = jax.random.uniform(jax.random.fold_in(_gk, 12), (212500, 64), jnp.float32, 0.0, 1)
        edge_weight = jax.random.uniform(jax.random.fold_in(_gk, 14), (212500,), jnp.float32, 0.0, 0.999998)
        return (x, src, dst, edge_attr_64, edge_weight)
    x, src, dst, edge_attr_64, edge_weight = _rec_inputs()

    def _L0_gnn_setup():
        import jax, jax.numpy as jnp
        import numpy as np
        N, E, D, K = (12500, 156250, 64, 64)
        key = jax.random.key(seed)
        ks = jax.random.split(key, 12)
        s = 1.0 / np.sqrt(D)
        return {'x': jax.random.normal(ks[0], (N, D), dtype=jnp.float32), 'i': jax.random.randint(ks[1], (E,), 0, N), 'j': jax.random.randint(ks[2], (E,), 0, N), 'rbf': jax.random.uniform(ks[3], (E, K), dtype=jnp.float32), 'Wf1': jax.random.uniform(ks[4], (D, K), jnp.float32, -s, s), 'bf1': jax.random.uniform(ks[5], (D,), jnp.float32, -s, s), 'Wf2': jax.random.uniform(ks[6], (D, D), jnp.float32, -s, s), 'bf2': jax.random.uniform(ks[7], (D,), jnp.float32, -s, s), 'Wl': jax.random.uniform(ks[8], (D, D), jnp.float32, -s, s), 'bl': jax.random.uniform(ks[9], (D,), jnp.float32, -s, s), 'gamma': jnp.ones((D,), jnp.float32), 'beta': jnp.zeros((D,), jnp.float32)}
    _L0_gnn_all = _L0_gnn_setup()
    _L0_gnn_in = {k: v for k, v in _L0_gnn_all.items() if k in ('Wf1', 'bf1', 'Wf2', 'bf2', 'Wl', 'bl', 'gamma', 'beta')}
    del _L0_gnn_all

    def _L1_gnn_setup():
        import jax, jax.numpy as jnp
        import numpy as np
        N_NODES = 6250
        N_EDGES = 100000
        D = 64
        key = jax.random.key(seed)
        ks = jax.random.split(key, 6)
        x = jax.random.normal(ks[0], (N_NODES, D), dtype=jnp.float32)
        edge_index = jax.random.randint(ks[1], (2, N_EDGES), 0, N_NODES, dtype=jnp.int64)
        edge_weight = jax.random.uniform(ks[2], (N_EDGES,), dtype=jnp.float32)
        s = 1.0 / np.sqrt(D)
        W1 = jax.random.normal(ks[3], (D, D), dtype=jnp.float32) * s
        b1 = jnp.zeros((D,), dtype=jnp.float32)
        W2 = jax.random.normal(ks[4], (D, D), dtype=jnp.float32) * s
        b2 = jnp.zeros((D,), dtype=jnp.float32)
        return {'x': x, 'edge_index': edge_index, 'edge_weight': edge_weight, 'W1': W1, 'b1': b1, 'W2': W2, 'b2': b2}
    _L1_gnn_all = _L1_gnn_setup()
    _L1_gnn_in = {k: v for k, v in _L1_gnn_all.items() if k in ('W1', 'b1', 'W2', 'b2')}
    del _L1_gnn_all
    return {'x': x, 'src': src, 'dst': dst, 'edge_attr_64': edge_attr_64, 'edge_weight': edge_weight, 'L0_gnn_Wf1': _L0_gnn_in['Wf1'], 'L0_gnn_bf1': _L0_gnn_in['bf1'], 'L0_gnn_Wf2': _L0_gnn_in['Wf2'], 'L0_gnn_bf2': _L0_gnn_in['bf2'], 'L0_gnn_Wl': _L0_gnn_in['Wl'], 'L0_gnn_bl': _L0_gnn_in['bl'], 'L0_gnn_gamma': _L0_gnn_in['gamma'], 'L0_gnn_beta': _L0_gnn_in['beta'], 'L1_gnn_W1': _L1_gnn_in['W1'], 'L1_gnn_b1': _L1_gnn_in['b1'], 'L1_gnn_W2': _L1_gnn_in['W2'], 'L1_gnn_b2': _L1_gnn_in['b2']}

def reference(x, src, dst, edge_attr_64, edge_weight, L0_gnn_Wf1, L0_gnn_bf1, L0_gnn_Wf2, L0_gnn_bf2, L0_gnn_Wl, L0_gnn_bl, L0_gnn_gamma, L0_gnn_beta, L1_gnn_W1, L1_gnn_b1, L1_gnn_W2, L1_gnn_b2):
    import jax
    import jax.numpy as jnp

    def _L0_gnn_ref(x, i, j, rbf, Wf1, bf1, Wf2, bf2, Wl, bl, gamma, beta):
        import jax, jax.numpy as jnp
        import numpy as np
        N, E, D, K = (12500, 156250, 64, 64)
        Wxh = x @ Wl.T + bl
        h = jax.nn.silu(rbf @ Wf1.T + bf1)
        f_ij = h @ Wf2.T + bf2
        msg = f_ij * Wxh[j]
        agg = jax.ops.segment_sum(msg, i, num_segments=x.shape[0])
        y = x + agg
        mu = jnp.mean(y, axis=-1, keepdims=True)
        var = jnp.var(y, axis=-1, keepdims=True)
        return (y - mu) * jax.lax.rsqrt(var + 1e-05) * gamma + beta

    def _L1_gnn_ref(x, edge_index, edge_weight, W1, b1, W2, b2):
        import jax, jax.numpy as jnp
        import numpy as np
        N_NODES = 6250
        N_EDGES = 100000
        D = 64
        src = edge_index[0]
        dst = edge_index[1]
        msg = x[src] * edge_weight[:, None]
        agg = jax.ops.segment_sum(msg, dst, num_segments=x.shape[0])
        h = agg + x
        h = jax.nn.relu(h @ W1 + b1)
        return h @ W2 + b2
    edge_index = jnp.stack([src, dst])
    x = _layernorm(x + _L0_gnn_ref(x, src, dst, edge_attr_64, L0_gnn_Wf1, L0_gnn_bf1, L0_gnn_Wf2, L0_gnn_bf2, L0_gnn_Wl, L0_gnn_bl, L0_gnn_gamma, L0_gnn_beta), axis=-1)
    x = _layernorm(x + _L1_gnn_ref(x, edge_index, edge_weight, L1_gnn_W1, L1_gnn_b1, L1_gnn_W2, L1_gnn_b2), axis=-1)
    return x

_drawn_inputs = setup_inputs


def setup_inputs(seed=0):
    import zlib

    import numpy as np

    out = dict(_drawn_inputs(seed))
    spreads = {'L0_gnn_gamma': (1.0, 0.2),
     'L0_gnn_beta': (0.0, 0.1),
     'L1_gnn_b1': (0.0, 0.1),
     'L1_gnn_b2': (0.0, 0.1)}
    factors = {}
    for name, (base, spread) in spreads.items():
        noise = np.random.default_rng([zlib.crc32(name.encode()), seed]).standard_normal(out[name].shape)
        drawn = base * np.exp(spread * noise) if base else spread * noise
        out[name] = jnp.asarray(drawn.astype(out[name].dtype))
    for name, factor in factors.items():
        out[name] = (out[name] * factor).astype(out[name].dtype)
    return out
```

```python
from contextlib import ExitStack

import concourse.bass as bass
from concourse import mybir

F32 = mybir.dt.float32
BF16 = mybir.dt.bfloat16
I32 = mybir.dt.int32
ALU = mybir.AluOpType
ACT = mybir.ActivationFunctionType
AX = mybir.AxisListType

P = 128
D = 64
T = 8
TQ = 4
ROWS_Q = TQ * P
W = D + 1
FAR = float(1 << 20)


def sizes(n_nodes, n_edges):
    blocks = -(-n_nodes // P)
    blocks_padded = -(-blocks // T) * T
    groups = -(-n_edges // (P * T))
    groups += groups % 2
    q_groups = (n_edges + blocks * (ROWS_Q - 1)) // ROWS_Q
    q_groups = -(-q_groups // 8) * 8
    return blocks, blocks_padded, groups, q_groups


def program(nc, n_nodes, n_edges, x, src, dst, ew, rbf, w, out, wxh_rows, x1_rows, sorted_rows, q_block_row, seed_rows):
    NB, NBP, NG, NQ = sizes(n_nodes, n_edges)
    NT = NG * T
    HALF = (T // 2) * NB
    assert HALF * 4 <= 2048 and NBP >= NB + 1
    QC = -(-NQ // P)
    FR = 32 if 32 * W <= NBP * D else 8
    FILL = sorted_rows.shape[0] // (P * FR)

    ctx = ExitStack()
    with ctx:
        def sb(name, shape, dt=F32):
            return ctx.enter_context(nc.sbuf_tensor(name, shape, dt))

        def pb(name, shape):
            return ctx.enter_context(nc.psum_tensor(name, shape, F32))

        def sem(name):
            return ctx.enter_context(nc.semaphore(name))

        def sem2(name):
            return [sem(f"{name}_{u}") for u in range(2)]

        xs = sb("xs", [P, NBP, D])
        agg = sb("agg", [P, NBP, D])
        x1 = sb("x1", [P, NBP, D])
        tmp = sb("tmp", [P, NBP, D])
        src_i = sb("src_i", [P, NT], I32)
        dst_i = sb("dst_i", [P, NT], I32)
        ew_s = sb("ew_s", [P, NT])
        hi_s = sb("hi_s", [P, NT], BF16)
        lo_s = sb("lo_s", [P, NT], BF16)
        hi_d = sb("hi_d", [P, NT], BF16)
        lo_d = sb("lo_d", [P, NT], BF16)
        far = sb("far", [P, NT], BF16)
        shifted = sb("shifted", [P, NT], I32)
        iota_i = sb("iota_i", [P, P], I32)
        iota = sb("iota", [P, P], BF16)
        iota_f = sb("iota_f", [P, P])
        ident = sb("ident", [P, P])
        ones = sb("ones", [P, P], BF16)
        tri = sb("tri", [P, P], BF16)
        zeros = sb("zeros", [P, HALF], BF16)
        onehot = sb("onehot", [P, T, NB], BF16)
        onehot2 = sb("onehot2", [P, T, NB], BF16)
        rank = sb("rank", [P, T, NB])
        run = sb("run", [P, NB])
        cnt = [sb(f"cnt{k}", [P, NB]) for k in range(3)]
        cnt_i = sb("cnt_i", [P, NB], I32)
        rank8 = sb("rank8", [P, T])
        pos = [sb(f"pos{u}", [P, T], I32) for u in range(2)]
        gidx = [sb(f"gidx{u}", [P, T], I32) for u in range(2)]
        gathered = [sb(f"gathered{u}", [P, T, D]) for u in range(2)]
        rows = [sb(f"rows{u}", [P, T, W]) for u in range(2)]
        rbf_s = [sb(f"rbf_s{u}", [P, T * D]) for u in range(2)]
        in_t = sb("in_t", [P, T * D])
        hid_t = sb("hid_t", [P, T * D])
        f_s = sb("f_s", [P, T, D])
        q_rows = [sb(f"q_rows{u}", [P, 4, TQ, W]) for u in range(2)]
        q_onehot = [sb(f"q_onehot{u}", [P, TQ, P]) for u in range(2)]
        q_num_i = sb("q_num_i", [P, QC], I32)
        q_num = sb("q_num", [P, QC])
        q_cmp = sb("q_cmp", [P, QC, NB])
        q_blk = sb("q_blk", [P, QC])
        q_blk_i = sb("q_blk_i", [P, QC], I32)
        q_row = sb("q_row", [1, QC * P], I32)
        stat = [sb(f"stat{k}", [P, NB]) for k in range(2)]
        eps = sb("eps", [P, 1])
        wts = {k: sb(f"w_{k}", list(a.shape)) for k, a in w.items()}

        ps_t = pb("ps_t", [P, T * D])
        ps_h = pb("ps_h", [P, T * D])
        ps_f = pb("ps_f", [P, T * D])
        ps_rank = pb("ps_rank", [P, 2, 512])
        ps_cnt = pb("ps_cnt", [P, 512])
        ps_agg = [pb(f"ps_agg{u}", [P, 512]) for u in range(2)]

        def before(u, i):
            return (1 - u, i + (u + 1))

        def seed(e, *pairs):
            for pair in pairs:
                for s in pair:
                    e.sem_inc(s, 1)

        s_const = sem("s_const")
        s_in = sem("s_in")
        s_x = sem("s_x")
        s_zero = sem("s_zero")
        s_fill = sem("s_fill")
        s_key = sem("s_key")
        w_t, w_ev, w_f, w_b, w_out = (sem(f"wxh_{k}") for k in ("t", "ev", "f", "b", "out"))

        with nc.Block() as block:
            @block.gpsimd
            def _(e):
                e.iota(iota_i[:, :], pattern=[[1, P]], base=0, channel_multiplier=0).then_inc(s_const, 1)
                e.iota(q_num_i[:, :], pattern=[[P, QC]], base=0, channel_multiplier=1).then_inc(s_const, 1)
                e.memset(ident[:, :], 0.0).then_inc(s_const, 1)
                e.memset(ones[:, :], 1.0).then_inc(s_const, 1)
                e.memset(zeros[:, :], 0.0).then_inc(s_const, 1)
                e.memset(eps[:, :], 1e-5).then_inc(s_const, 1)
                e.wait_ge(s_const, 6)
                e.affine_select(out=ident[:, :], in_=ident[:, :], compare_op=ALU.not_equal, fill=1.0,
                                base=0, pattern=[[-1, P]], channel_multiplier=1).then_inc(s_const, 1)
                e.affine_select(out=tri[:, :], in_=ones[:, :], compare_op=ALU.is_gt, fill=0.0,
                                base=0, pattern=[[1, P]], channel_multiplier=-1).then_inc(s_const, 1)

            @block.sync
            def _(e):
                e.dma_start(xs[:, :, :], x.rearrange("(b p) d -> p b d", p=P)).then_inc(s_x, 16)
                for t, a in ((src_i, src), (dst_i, dst), (ew_s, ew)):
                    e.dma_start(t[:, :], a).then_inc(s_in, 16)
                e.wait_ge(s_zero, 1)
                z = agg[:, :, :].rearrange("p b d -> p (b d)")[:, 0:FR * W]
                fill = sorted_rows.rearrange("(c p r) w -> c p (r w)", p=P, r=FR)
                with e.Fori(0, FILL) as c:
                    e.dma_start(fill[bass.ds(c, 1), :, :].rearrange("c p n -> (c p) n"), z).then_inc(s_fill, 16)
                e.wait_ge(s_fill, 16 * FILL)

            @block.scalar
            def _(e):
                for k, a in w.items():
                    e.dma_start(wts[k][:, :], a).then_inc(w_b, 16)
                for g in range(NBP // T):
                    e.wait_ge(w_t, g + 1)
                    e.wait_ge(w_f, g)
                    e.activation(in_t[:, :], ps_t[:, :], ACT.Copy).then_inc(w_ev, 1)
                e.wait_ge(w_out, 16)

            @block.tensor
            def _(e):
                e.wait_ge(s_const, 8)
                e.wait_ge(s_x, 16)
                e.wait_ge(w_b, 16 * len(w))
                for g in range(NBP // T):
                    e.wait_ge(w_ev, g)
                    for k in range(T // 2):
                        pair = xs[:, g * T + 2 * k:g * T + 2 * k + 2, :].rearrange("p b d -> p (b d)")
                        last = e.transpose(ps_t[:, k * P:(k + 1) * P], pair, ident[:, :])
                    last.then_inc(w_t, 1)
                    e.wait_ge(w_ev, g + 1)
                    e.wait_ge(s_key, g)
                    for k in range(T // 2):
                        last = e.matmul(ps_f[:, k * P:(k + 1) * P], in_t[:, k * P:(k + 1) * P],
                                        wts["wl"][:, :], start=True, stop=True)
                    last.then_inc(w_f, 1)

            s_d = sem("s_d")

            @block.vector
            def _(e):
                e.memset(agg[:, :, :], 0.0).then_inc(s_zero, 1)
                e.wait_ge(s_const, 8)
                e.tensor_copy(iota[:, :], iota_i[:, :]).then_inc(s_d, 1)
                e.tensor_copy(iota_f[:, :], iota_i[:, :]).then_inc(s_d, 1)
                e.tensor_copy(q_num[:, :], q_num_i[:, :]).then_inc(s_d, 1)
                e.wait_ge(s_in, 48)
                n = 3
                for a, hi, lo in ((src_i, hi_s, lo_s), (dst_i, hi_d, lo_d)):
                    e.wait_ge(s_d, n)
                    e.tensor_scalar(shifted[:, :], a[:, :], 7, None, ALU.logical_shift_right).then_inc(s_d, 1)
                    e.wait_ge(s_d, n + 1)
                    e.tensor_copy(hi[:, :], shifted[:, :]).then_inc(s_d, 1)
                    e.wait_ge(s_d, n + 2)
                    e.tensor_scalar(shifted[:, :], a[:, :], P - 1, None, ALU.bitwise_and).then_inc(s_d, 1)
                    e.wait_ge(s_d, n + 3)
                    e.tensor_copy(lo[:, :], shifted[:, :]).then_inc(s_d, 1)
                    n += 4
                e.tensor_scalar(far[:, :], hi_s[:, :], float(NB), FAR, ALU.is_ge, ALU.mult).then_inc(s_d, 1)
                for g in range(NBP // T):
                    e.wait_ge(w_f, g + 1)
                    e.tensor_tensor(tmp[:, g * T:(g + 1) * T, :],
                                    ps_f[:, :].rearrange("p (t d) -> p t d", d=D),
                                    wts["bl"][:, None, :].broadcast_to([P, T, D]), ALU.add).then_inc(s_key, 1)

            @block.gpsimd
            def _(e):
                e.wait_ge(s_key, NBP // T)
                e.dma_start(wxh_rows.rearrange("(b p) d -> p b d", p=P), tmp[:, 0:NB, :]).then_inc(w_out, 16)

        def count(layer, hi):
            c_oh, c_mm = sem2(f"c{layer}_oh"), sem2(f"c{layer}_mm")
            c_zero, c_tot, c_d, c_dma, c_dma2 = (sem(f"c{layer}_{k}") for k in ("zero", "tot", "d", "dma", "dma2"))
            oh = [onehot, onehot2]
            with nc.Block() as block:
                @block.vector
                def _(e):
                    with e.Fori(0, NG // 2) as i:
                        for u in range(2):
                            e.wait_ge(c_mm[u], i + 1)
                            e.tensor_tensor(
                                oh[u][:, :, :],
                                hi[:, bass.ds(i * (2 * T) + u * T, T)].unsqueeze(2).broadcast_to([P, T, NB]),
                                iota[:, None, 0:NB].broadcast_to([P, T, NB]), ALU.is_equal).then_inc(c_oh[u], 1)
                    e.wait_ge(c_tot, 1)
                    n = 0

                    def step(ins):
                        nonlocal n
                        ins.then_inc(c_d, 1)
                        n += 1
                        e.wait_ge(c_d, n)

                    step(e.tensor_reduce(cnt[0][:, :], ps_cnt[:, 0:HALF].rearrange("p (t b) -> p b t", b=NB),
                                         AX.X, ALU.add))
                    step(e.tensor_scalar(cnt[0][:, :], cnt[0][:, :], float(ROWS_Q - 1), None, ALU.add))
                    step(e.tensor_copy(cnt_i[:, :], cnt[0][:, :]))
                    step(e.tensor_scalar(cnt_i[:, :], cnt_i[:, :], ROWS_Q.bit_length() - 1, None,
                                         ALU.logical_shift_right))
                    step(e.tensor_copy(cnt[0][:, :], cnt_i[:, :]))
                    a, b = cnt[1], cnt[2]
                    step(e.tensor_copy(a[:, :], cnt[0][:, :]))
                    k = 1
                    while k < NB:
                        step(e.tensor_copy(b[:, 0:k], a[:, 0:k]))
                        step(e.tensor_tensor(b[:, k:NB], a[:, k:NB], a[:, 0:NB - k], ALU.add))
                        a, b = b, a
                        k *= 2
                    step(e.tensor_tensor(
                        q_cmp[:, :, :], a[:, None, :].broadcast_to([P, QC, NB]),
                        q_num[:, :].unsqueeze(2).broadcast_to([P, QC, NB]), ALU.is_le))
                    step(e.tensor_reduce(q_blk[:, :], q_cmp[:, :, :], AX.X, ALU.add))
                    step(e.tensor_copy(q_blk_i[:, :], q_blk[:, :]))
                    step(e.tensor_tensor(b[:, :], a[:, :], cnt[0][:, :], ALU.subtract))
                    step(e.tensor_scalar(run[:, :], b[:, :], float(ROWS_Q), None, ALU.mult))
                    e.sem_inc(c_d, 1)

                n_steps = 6 + 2 * (NB - 1).bit_length() + 5 + 1

                @block.tensor
                def _(e):
                    seed(e, c_mm)
                    e.matmul(ps_cnt[:, 0:HALF], ones[:, :], zeros[:, :], start=True, stop=False).then_inc(c_zero, 1)
                    with e.Fori(0, NG // 2) as i:
                        for u in range(2):
                            e.wait_ge(c_oh[u], i + 1)
                            for h in range(2):
                                last = e.matmul(ps_cnt[:, 0:HALF], ones[:, :],
                                                oh[u][:, h * (T // 2):(h + 1) * (T // 2), :].rearrange("p t b -> p (t b)"),
                                                start=False, stop=False)
                            last.then_inc(c_mm[u], 1)
                    e.matmul(ps_cnt[:, 0:HALF], ones[:, :], zeros[:, :], start=False, stop=True).then_inc(c_tot, 1)

                @block.sync
                def _(e):
                    e.wait_ge(c_d, n_steps)
                    with nc.allow_non_contiguous_dma(reason="a few hundred words"):
                        e.dma_start(q_block_row[0, :].rearrange("(c p) -> p c", p=P), q_blk_i[:, :]).then_inc(c_dma, 16)
                    e.wait_ge(c_dma, 16)
                    e.dma_start(q_row[:, :], q_block_row).then_inc(c_dma2, 16)
                    e.wait_ge(c_dma2, 16)

        def messages(layer, hi, lo, idx, table):
            n_ = f"m{layer}_"
            gi, xg, m, lo_w, sc = (sem2(n_ + k) for k in ("gi", "xg", "m", "lo", "sc"))
            oh, rk, vv, rn, ww, pr, po = (sem2(n_ + k) for k in ("oh", "rk", "vv", "rn", "ww", "pr", "po"))
            if layer == 0:
                ld, tr, ev, h1, si, f2, f1 = (sem2(n_ + k) for k in ("ld", "tr", "ev", "h1", "si", "f2", "f1"))
            with nc.Block() as block:
                if layer == 0:
                    @block.sync
                    def _(e):
                        r = rbf.rearrange("(g p t) k -> g p (t k)", p=P, t=T)
                        with e.Fori(0, NG // 2) as i:
                            for u in range(2):
                                e.wait_ge(tr[u], i + 1)
                                e.dma_start(rbf_s[u][:, :], r[bass.ds(i * 2 + u, 1), :, :].rearrange("g p n -> (g p) n")
                                            ).then_inc(ld[u], 16)
                        for u in range(2):
                            e.wait_ge(ld[u], 16 * (NG // 2))

                    @block.scalar
                    def _(e):
                        seed(e, ev, si)
                        with e.Fori(0, NG // 2) as i:
                            for u in range(2):
                                v, k = before(u, i)
                                e.wait_ge(h1[v], k)
                                e.wait_ge(tr[u], i + 2)
                                e.activation(in_t[:, :], ps_t[:, :], ACT.Copy).then_inc(ev[u], 1)
                                e.wait_ge(sc[u], i * (16 * T) + 16 * T)
                                e.activation(rows[u][:, :, D], lo[:, bass.ds(i * (2 * T) + u * T, T)],
                                             ACT.Copy).then_inc(lo_w[u], 1)
                                e.wait_ge(f2[v], k)
                                e.wait_ge(h1[u], i + 2)
                                e.activation(hid_t[:, :], ps_h[:, :], ACT.Silu,
                                             bias=wts["bf1"][:, 0:1]).then_inc(si[u], 1)
                else:
                    @block.scalar
                    def _(e):
                        with e.Fori(0, NG // 2) as i:
                            for u in range(2):
                                e.wait_ge(sc[u], i * (16 * T) + 16 * T)
                                e.activation(rows[u][:, :, D], lo[:, bass.ds(i * (2 * T) + u * T, T)],
                                             ACT.Copy).then_inc(lo_w[u], 1)

                @block.tensor
                def _(e):
                    seed(e, rk, *((tr, h1, f2) if layer == 0 else ()))
                    with e.Fori(0, NG // 2) as i:
                        for u in range(2):
                            v, k = before(u, i)
                            if layer == 0:
                                e.wait_ge(ld[u], i * 16 + 16)
                                e.wait_ge(ev[v], k)
                                for t in range(T // 2):
                                    last = e.transpose(ps_t[:, t * P:(t + 1) * P],
                                                       rbf_s[u][:, t * P:(t + 1) * P], ident[:, :])
                                last.then_inc(tr[u], 1)
                            e.wait_ge(vv[v], k)
                            e.wait_ge(rn[v], k)
                            e.wait_ge(oh[u], i + 1)
                            for h in range(2):
                                t0 = h * (T // 2)
                                bank = ps_rank[:, h, 0:HALF]
                                e.matmul(bank, tri[:, :], onehot[:, t0:t0 + T // 2, :].rearrange("p t b -> p (t b)"),
                                         start=True, stop=False)
                                for t in range(t0 + T // 2 - 1):
                                    f = max(t + 1, t0)
                                    e.matmul(ps_rank[:, h, (f - t0) * NB:HALF].rearrange("p (t b) -> p t b", b=NB),
                                             ones[:, :],
                                             onehot[:, t:t + 1, :].broadcast_to([P, t0 + T // 2 - f, NB]),
                                             start=False, stop=(t == t0 + T // 2 - 2))
                            for t in range(T):
                                last = e.matmul(ps_cnt[:, 0:NB], ones[:, :], onehot[:, t, :],
                                                start=(t == 0), stop=(t == T - 1))
                            last.then_inc(rk[u], 1)
                            if layer == 0:
                                e.wait_ge(si[v], k)
                                e.wait_ge(ev[u], i + 2)
                                e.matmul(ps_h[:, :], wts["wf1"][:, :], in_t[:, :], start=True, stop=True).then_inc(h1[u], 1)
                                e.wait_ge(f1[v], k)
                                e.wait_ge(si[u], i + 2)
                                for t in range(T // 2):
                                    last = e.matmul(ps_f[:, t * P:(t + 1) * P], hid_t[:, t * P:(t + 1) * P],
                                                    wts["wf2"][:, :], start=True, stop=True)
                                last.then_inc(f2[u], 1)

                @block.vector
                def _(e):
                    seed(e, vv, rn, ww, pr, po, m, *((f1,) if layer == 0 else ()))
                    with e.Fori(0, NG // 2) as i:
                        for u in range(2):
                            v, k = before(u, i)
                            at = bass.ds(i * (2 * T) + u * T, T)
                            e.wait_ge(m[u], i + 1)
                            e.tensor_copy(gidx[u][:, :], idx[:, at]).then_inc(gi[u], 1)
                            e.wait_ge(rk[v], k)
                            e.wait_ge(ww[v], k)
                            e.tensor_tensor(onehot[:, :, :], hi[:, at].unsqueeze(2).broadcast_to([P, T, NB]),
                                            iota[:, None, 0:NB].broadcast_to([P, T, NB]), ALU.is_equal).then_inc(oh[u], 1)
                            e.wait_ge(pr[v], k)
                            e.wait_ge(rn[v], k)
                            e.wait_ge(rk[u], i + 2)
                            e.tensor_tensor(rank[:, :, :].rearrange("p (h t) b -> p h t b", h=2),
                                            ps_rank[:, :, 0:HALF].rearrange("p h (t b) -> p h t b", b=NB),
                                            run[:, None, None, :].broadcast_to([P, 2, T // 2, NB]), ALU.add).then_inc(vv[u], 1)
                            e.wait_ge(vv[u], i + 2)
                            e.tensor_tensor(run[:, :], run[:, :], ps_cnt[:, 0:NB], ALU.add).then_inc(rn[u], 1)
                            e.tensor_tensor(rank[:, :, :], rank[:, :, :], onehot[:, :, :], ALU.mult).then_inc(ww[u], 1)
                            e.wait_ge(po[v], k)
                            e.wait_ge(ww[u], i + 2)
                            e.tensor_reduce(rank8[:, :], rank[:, :, :], AX.X, ALU.add).then_inc(pr[u], 1)
                            e.wait_ge(sc[u], i * (16 * T) + 16 * T)
                            e.wait_ge(pr[u], i + 2)
                            e.tensor_tensor(pos[u][:, :], rank8[:, :], far[:, at], ALU.add).then_inc(po[u], 1)
                            if layer == 0:
                                e.wait_ge(m[v], k)
                                e.wait_ge(f2[u], i + 2)
                                e.tensor_tensor(f_s[:, :, :], ps_f[:, :].rearrange("p (t d) -> p t d", d=D),
                                                wts["bf2"][:, None, :].broadcast_to([P, T, D]), ALU.add).then_inc(f1[u], 1)
                                e.wait_ge(f1[u], i + 2)
                            e.wait_ge(xg[u], i * (16 * T) + 16 * T)
                            other = f_s[:, :, :] if layer == 0 else ew_s[:, at].unsqueeze(2).broadcast_to([P, T, D])
                            e.tensor_tensor(rows[u][:, :, 0:D], gathered[u][:, :, :], other, ALU.mult).then_inc(m[u], 1)

                @block.gpsimd
                def _(e):
                    def gather(u, i):
                        e.wait_ge(m[u], i + 1)
                        e.wait_ge(gi[u], i + 1)
                        e.sem_inc(s_go, 1)
                        for t in range(T):
                            e.indirect_dma_start(
                                out=gathered[u][:, t, :], out_offset=None, in_=table,
                                in_offset=bass.IndirectOffsetOnAxis(ap=gidx[u][:, t:t + 1], axis=0),
                                bounds_check=n_nodes - 1, oob_is_err=False).then_inc(xg[u], 16)

                    def scatter(u, i):
                        e.wait_ge(m[u], i + 2)
                        e.wait_ge(lo_w[u], i + 1)
                        e.wait_ge(po[u], i + 2)
                        e.sem_inc(s_go, 1)
                        for t in range(T):
                            e.indirect_dma_start(
                                out=sorted_rows, out_offset=bass.IndirectOffsetOnAxis(ap=pos[u][:, t:t + 1], axis=0),
                                in_=rows[u][:, t, :], in_offset=None,
                                bounds_check=NQ * ROWS_Q - 1, oob_is_err=False).then_inc(sc[u], 16)

                    for u in range(2):
                        e.memset(gathered[u][:, :, :], 0.0).then_inc(s_pad, 1)
                    e.wait_ge(s_pad, 2 * (layer + 1))
                    for u in range(2):
                        e.dma_start(seed_rows[u:u + 1, :], zeros[0:1, 0:16]).then_inc(sc[u], 16 * T)
                    gather(0, 0)
                    with e.Fori(0, NG // 2 - 1) as i:
                        gather(1, i)
                        scatter(0, i)
                        gather(0, i + 1)
                        scatter(1, i)
                    i = NG // 2 - 1
                    gather(1, i)
                    scatter(0, i)
                    scatter(1, i)
                    for u in range(2):
                        e.wait_ge(sc[u], 16 * T * (NG // 2 + 1))

        def reduce_rows(layer):
            n_ = f"r{layer}_"
            ld, used = sem2(n_ + "ld"), sem2(n_ + "used")
            oh, mm, ac = (sem2(n_ + k) for k in ("oh", "mm", "ac"))

            def products(q, i):
                if q % 4 == 3:
                    return used[q // 4], i + 2
                if q % 2:
                    return mm[1], i * 2 + (q // 4 + 2)
                return mm[0], i * 4 + (q // 2 + 2)

            with nc.Block() as block:
                @block.sync
                def _(e):
                    r = sorted_rows.rearrange("(c q p t) w -> c p q (t w)", q=4, p=P, t=TQ)
                    with e.Fori(0, NQ // 8) as i:
                        for u in range(2):
                            e.wait_ge(used[u], i + 1)
                            e.dma_start(q_rows[u][:, :, :, :].rearrange("p q t w -> p q (t w)"),
                                        r[bass.ds(i * 2 + u, 1), :, :, :].rearrange("c p q n -> (c p) q n")).then_inc(ld[u], 16)
                    for u in range(2):
                        e.wait_ge(ld[u], 16 * (NQ // 8))

                @block.tensor
                def _(e):
                    seed(e, mm, used)
                    with e.Fori(0, NQ // 8) as i:
                        for q in range(8):
                            u, s, k = q // 4, q % 2, q // 2
                            e.wait_ge(ac[s], i * 4 + (k + 1))
                            e.wait_ge(oh[s], i * 4 + k + 1)
                            for t in range(TQ):
                                last = e.matmul(ps_agg[s][:, 0:D], q_onehot[s][:, t, :], q_rows[u][:, q % 4, t, 0:D],
                                                start=(t == 0), stop=(t == TQ - 1))
                            last.then_inc(products(q, i)[0], 1)

                @block.vector
                def _(e):
                    seed(e, ac)
                    with e.Fori(0, NQ // 8) as i:
                        for q in range(9):
                            if q < 8:
                                u, s, k = q // 4, q % 2, q // 2
                                if q % 4 == 0:
                                    e.wait_ge(ld[u], i * 16 + 16)
                                e.wait_ge(*((mm[0], i * 4 + 1), (used[1], i + 1))[q] if q < 2 else products(q - 2, i))
                                e.tensor_tensor(q_onehot[s][:, :, :],
                                                q_rows[u][:, q % 4, :, D:D + 1].broadcast_to([P, TQ, P]),
                                                iota_f[:, None, :].broadcast_to([P, TQ, P]), ALU.is_equal).then_inc(oh[s], 1)
                            if q > 0:
                                s, k = (q - 1) % 2, (q - 1) // 2
                                b = e.value_load(q_row[0:1, bass.ds(i * 8 + (q - 1), 1)], min_val=0, max_val=NB)
                                e.wait_ge(*products(q - 1, i))
                                e.wait_ge(ac[1 - s], i * 4 + (k + s + 1))
                                to = agg[:, bass.ds(b, 1), :].rearrange("p b d -> p (b d)")
                                e.tensor_tensor(to, to, ps_agg[s][:, 0:D], ALU.add).then_inc(ac[s], 1)

        def norm_steps(e, step, to, of, square, s_act, s_var, nth):
            bc = lambda a: a[:, :].unsqueeze(2).broadcast_to([P, NB, D])
            step(e.tensor_reduce(stat[0][:, :], of, AX.X, ALU.add))
            step(e.tensor_scalar(stat[0][:, :], stat[0][:, :], 1.0 / D, None, ALU.mult))
            step(e.tensor_tensor(to, of, bc(stat[0]), ALU.subtract))
            step(e.tensor_tensor(square, to, to, ALU.mult))
            step(e.tensor_reduce(stat[0][:, :], square, AX.X, ALU.add))
            e.sem_inc(s_var, 1)
            e.wait_ge(s_act, nth)
            step(e.reciprocal(stat[0][:, :], stat[1][:, :]))
            step(e.tensor_tensor(to, to, bc(stat[0]), ALU.mult))

        def root(e, s_act, s_var, nth):
            e.wait_ge(s_var, nth)
            e.activation(stat[1][:, :], stat[0][:, :], ACT.Sqrt, scale=1.0 / D, bias=eps[:, 0:1]).then_inc(s_act, 1)

        def stepper(e, s):
            n = [0]

            def step(ins):
                ins.then_inc(s, 1)
                n[0] += 1
                e.wait_ge(s, n[0])
            return step

        def node_update():
            d_, a_, v_, done, o_ = (sem(f"n0_{k}") for k in ("d", "a", "v", "done", "o"))
            A, X, X1, Y = (t[:, 0:NB, :] for t in (agg, xs, x1, tmp))
            bc = lambda a: a[:, None, :].broadcast_to([P, NB, D])
            with nc.Block() as block:
                @block.vector
                def _(e):
                    step = stepper(e, d_)
                    step(e.memset(x1[:, NB:NBP, :], 0.0))
                    step(e.tensor_tensor(A, A, X, ALU.add))
                    norm_steps(e, step, A, A, Y, a_, v_, 1)
                    step(e.tensor_tensor(A, A, bc(wts["gamma"]), ALU.mult))
                    step(e.tensor_tensor(A, A, bc(wts["beta"]), ALU.add))
                    step(e.tensor_tensor(A, A, X, ALU.add))
                    norm_steps(e, step, X1, A, Y, a_, v_, 2)
                    e.sem_inc(done, 1)
                    step(e.memset(agg[:, :, :], 0.0))

                @block.scalar
                def _(e):
                    root(e, a_, v_, 1)
                    root(e, a_, v_, 2)

                @block.sync
                def _(e):
                    e.wait_ge(done, 1)
                    e.dma_start(x1_rows.rearrange("(b p) d -> p b d", p=P), X1).then_inc(o_, 16)
                    e.wait_ge(o_, 16)

        def refill():
            f_ = sem("refill")
            with nc.Block() as block:
                @block.sync
                def _(e):
                    z = agg[:, :, :].rearrange("p b d -> p (b d)")[:, 0:FR * W]
                    fill = sorted_rows.rearrange("(c p r) w -> c p (r w)", p=P, r=FR)
                    with e.Fori(0, FILL) as c:
                        e.dma_start(fill[bass.ds(c, 1), :, :].rearrange("c p n -> (c p) n"), z).then_inc(f_, 16)
                    e.wait_ge(f_, 16 * FILL)

        def node_mlp():
            d_, a_, v_, add, t_, ev, h1, re, f2, f1, o_ = (
                sem(f"n1_{k}") for k in ("d", "a", "v", "add", "t", "ev", "h1", "re", "f2", "f1", "o"))
            A, X1, Y = (t[:, 0:NB, :] for t in (agg, x1, tmp))
            G = NBP // T
            with nc.Block() as block:
                @block.vector
                def _(e):
                    step = stepper(e, d_)
                    step(e.tensor_tensor(agg[:, :, :], agg[:, :, :], x1[:, :, :], ALU.add))
                    e.sem_inc(add, 1)
                    for g in range(G):
                        e.wait_ge(f2, g + 1)
                        to = tmp[:, g * T:(g + 1) * T, :]
                        step(e.tensor_tensor(to, ps_f[:, :].rearrange("p (t d) -> p t d", d=D),
                                             x1[:, g * T:(g + 1) * T, :], ALU.add))
                        e.sem_inc(f1, 1)
                        step(e.tensor_tensor(to, to, wts["b2"][:, None, :].broadcast_to([P, T, D]), ALU.add))
                    norm_steps(e, step, Y, Y, A, a_, v_, 1)
                    e.sem_inc(add, 1)

                @block.tensor
                def _(e):
                    e.wait_ge(add, 1)
                    for g in range(G):
                        e.wait_ge(ev, g)
                        for k in range(T // 2):
                            pair = agg[:, g * T + 2 * k:g * T + 2 * k + 2, :].rearrange("p b d -> p (b d)")
                            last = e.transpose(ps_t[:, k * P:(k + 1) * P], pair, ident[:, :])
                        last.then_inc(t_, 1)
                        e.wait_ge(re, g)
                        e.wait_ge(ev, g + 1)
                        e.matmul(ps_h[:, :], wts["w1"][:, :], in_t[:, :], start=True, stop=True).then_inc(h1, 1)
                        e.wait_ge(f1, g)
                        e.wait_ge(re, g + 1)
                        for k in range(T // 2):
                            last = e.matmul(ps_f[:, k * P:(k + 1) * P], hid_t[:, k * P:(k + 1) * P],
                                            wts["w2"][:, :], start=True, stop=True)
                        last.then_inc(f2, 1)

                @block.scalar
                def _(e):
                    for g in range(G):
                        e.wait_ge(h1, g)
                        e.wait_ge(t_, g + 1)
                        e.activation(in_t[:, :], ps_t[:, :], ACT.Copy).then_inc(ev, 1)
                        e.wait_ge(f2, g)
                        e.wait_ge(h1, g + 1)
                        e.activation(hid_t[:, :], ps_h[:, :], ACT.Relu, bias=wts["b1"][:, 0:1]).then_inc(re, 1)
                    root(e, a_, v_, 1)

                @block.sync
                def _(e):
                    e.wait_ge(add, 2)
                    e.dma_start(out.rearrange("(b p) d -> p b d", p=P), Y).then_inc(o_, 16)
                    e.wait_ge(o_, 16)

        s_pad = sem("s_pad")
        s_go = sem("s_go")
        count(0, hi_s)
        messages(0, hi_s, lo_s, dst_i, wxh_rows)
        reduce_rows(0)
        node_update()
        refill()
        count(1, hi_d)
        messages(1, hi_d, lo_d, src_i, x1_rows)
        reduce_rows(1)
        node_mlp()


def kernel(x, src, dst, edge_attr_64, edge_weight, L0_gnn_Wf1, L0_gnn_bf1, L0_gnn_Wf2, L0_gnn_bf2, L0_gnn_Wl,
           L0_gnn_bl, L0_gnn_gamma, L0_gnn_beta, L1_gnn_W1, L1_gnn_b1, L1_gnn_W2, L1_gnn_b2):
    import concourse.bacc as bacc
    import numpy as np
    from concourse.bass_utils import run_bass_kernel_spmd

    x, src, dst, rbf, ew = (np.asarray(a) for a in (x, src, dst, edge_attr_64, edge_weight))
    n_nodes, n_edges = x.shape[0], src.shape[0]
    NB, NBP, NG, NQ = sizes(n_nodes, n_edges)
    pad_node = (2 * NB) * P

    def edges(a, fill):
        a = np.concatenate([a, np.full(NG * T * P - n_edges, fill, a.dtype)])
        return np.ascontiguousarray(a.reshape(NG, P, T).transpose(1, 0, 2).reshape(P, NG * T))

    def twice(a):
        a = np.asarray(a)
        z = np.zeros_like(a)
        return np.ascontiguousarray(np.block([[a, z], [z, a]]))

    def column(a):
        return np.ascontiguousarray(np.concatenate([a, a]).reshape(P, 1))

    def spread(a):
        return np.ascontiguousarray(np.broadcast_to(np.asarray(a), (P, D)))

    w = {
        "wf1": twice(np.asarray(L0_gnn_Wf1).T), "wf2": twice(np.asarray(L0_gnn_Wf2).T),
        "wl": twice(np.asarray(L0_gnn_Wl).T), "w1": twice(L1_gnn_W1), "w2": twice(L1_gnn_W2),
        "bf1": column(L0_gnn_bf1), "b1": column(L1_gnn_b1),
        "bf2": spread(L0_gnn_bf2), "bl": spread(L0_gnn_bl), "gamma": spread(L0_gnn_gamma),
        "beta": spread(L0_gnn_beta), "b2": spread(L1_gnn_b2),
    }
    arrays = {
        "x": np.concatenate([x, np.zeros((NBP * P - n_nodes, D), x.dtype)]),
        "src": edges(src, pad_node), "dst": edges(dst, pad_node), "ew": edges(ew, 0),
        "rbf": np.concatenate([rbf, np.zeros((NG * T * P - n_edges, D), rbf.dtype)]),
        **{f"w_{k}_dram": a for k, a in w.items()},
    }
    nc = bacc.Bacc("TRN2", target_bir_lowering=False, num_devices=1)
    ap = {k: nc.dram_tensor(k, a.shape, mybir.dt.from_np(a.dtype), kind="ExternalInput").ap() for k, a in arrays.items()}
    out = nc.dram_tensor("out", (NB * P, D), F32, kind="ExternalOutput").ap()
    wxh_rows = nc.dram_tensor("wxh_rows", (NB * P, D), F32).ap()
    x1_rows = nc.dram_tensor("x1_rows", (NB * P, D), F32).ap()
    sorted_rows = nc.dram_tensor("sorted_rows", (NQ * ROWS_Q, W), F32).ap()
    q_block_row = nc.dram_tensor("q_block_row", (1, -(-NQ // P) * P), I32).ap()
    seed_rows = nc.dram_tensor("seed_rows", (2, 16), BF16).ap()
    program(nc, n_nodes, n_edges, ap["x"], ap["src"], ap["dst"], ap["ew"], ap["rbf"],
            {k: ap[f"w_{k}_dram"] for k in w}, out, wxh_rows, x1_rows, sorted_rows, q_block_row, seed_rows)
    r = run_bass_kernel_spmd(nc, [arrays], core_ids=[0])
    return r.results[0]["out"][:n_nodes]
```

```python
from contextlib import ExitStack

import concourse.bass as bass
from concourse import mybir

F32 = mybir.dt.float32
BF16 = mybir.dt.bfloat16
I32 = mybir.dt.int32
ALU = mybir.AluOpType
ACT = mybir.ActivationFunctionType
AX = mybir.AxisListType

P = 128
D = 64
T = 8
S = 4
TQ = 4
ROWS_Q = TQ * P
PARTS = 3
W = D + 1
FAR = float(1 << 20)


def sizes(n_nodes, n_edges):
    blocks = -(-n_nodes // P)
    blocks_padded = -(-blocks // T) * T
    groups = -(-n_edges // (P * T))
    groups = -(-groups // S) * S
    q_groups = (n_edges + blocks * (ROWS_Q - 1)) // ROWS_Q
    q_groups = -(-q_groups // 8) * 8
    return blocks, blocks_padded, groups, q_groups


def program(nc, n_nodes, n_edges, x, src, dst, ew, rbf, w, out, wxh_rows, x1_rows, sorted_rows, q_block_row, seed_rows,
            rel_rows):
    NB, NBP, NG, NQ = sizes(n_nodes, n_edges)
    NT = NG * T
    HALF = (T // 2) * NB
    NC = -(-NT // P)
    NGC = -(-NG // P)
    assert HALF * 4 <= 2048 and NBP >= NB + 1
    QC = -(-NQ // P)
    FR = 32 if 32 * W <= NBP * D else 8
    FILL = sorted_rows.shape[0] // (P * FR)

    ctx = ExitStack()
    with ctx:
        def sb(name, shape, dt=F32):
            return ctx.enter_context(nc.sbuf_tensor(name, shape, dt))

        def pb(name, shape):
            return ctx.enter_context(nc.psum_tensor(name, shape, F32))

        def sem(name):
            return ctx.enter_context(nc.semaphore(name))

        def sem2(name):
            return [sem(f"{name}_{u}") for u in range(2)]

        shared = {}

        def shared_sem(name):
            if name not in shared:
                shared[name] = sem(name)
            return shared[name]

        def shared_sem2(name):
            return [shared_sem(f"{name}_{u}") for u in range(2)]

        buffers = max(S * T * (W + D) + S * T * D, 4 * TQ * (PARTS * D + 2 * D + P // 2))
        spaces = [sb(name, [P, max(NBP * D, buffers)]) for name in ("x1_space", "x_space")]
        x1, xs = (a[:, 0:NBP * D].rearrange("p (b d) -> p b d", d=D) for a in spaces)
        agg = sb("agg", [P, NBP, D])

        def carve(layer, *shapes):
            at, found = 0, []
            for n, *dims in shapes:
                size = 1
                for d in dims:
                    size *= d
                names = "abc"[:len(dims)]
                for _ in range(n):
                    a = spaces[layer][:, at:at + size]
                    found.append(a.rearrange(f"p ({' '.join(names)}) -> p {' '.join(names)}",
                                             **dict(zip(names, dims))))
                    at += size
            assert at <= spaces[layer].shape[1]
            return found

        tmp_space = sb("tmp_space", [P, max(NBP * PARTS * D // 2, 8 * TQ * W)])
        tmp = tmp_space[:, 0:NBP * D].rearrange("p (b d) -> p b d", d=D)
        wxh = tmp_space[:, 0:NBP * PARTS * D // 2].bitcast(BF16).rearrange("p (b c d) -> p b c d", c=PARTS, d=D)
        src_i = sb("src_i", [P, NT], I32)
        dst_i = sb("dst_i", [P, NT], I32)
        ew_s = sb("ew_s", [P, NT])
        hi_s = sb("hi_s", [P, NT], BF16)
        lo_s = sb("lo_s", [P, NT], BF16)
        hi_d = sb("hi_d", [P, NT], BF16)
        lo_d = sb("lo_d", [P, NT], BF16)
        far = sb("far", [P, NT], BF16)
        rel = sb("rel", [P, NC * P], BF16)
        rel_bc = [sb(f"rel_bc{u}", [P, T * P], BF16) for u in range(2)]
        window = sb("window", [P, 2 * T * P], BF16)
        window_t = window[:, :].rearrange("p (h n) -> p h n", h=2)
        window_e = window[:, :].rearrange("p (t n) -> p t n", t=T)
        node_iota = sb("node_iota", [P, 2])
        node_iota_i = sb("node_iota_i", [P, 2], I32)
        iota = sb("iota", [P, 2 * P], BF16)
        ident = sb("ident", [P, P])
        ident_b = sb("ident_b", [P, P], BF16)
        ones = sb("ones", [P, P], BF16)
        ones_f = sb("ones_f", [P, P])
        tri = sb("tri", [P, P], BF16)
        before8 = sb("before8", [P, T, T], BF16)
        zeros = sb("zeros", [P, HALF], BF16)
        onehot = [sb(f"onehot{u}", [P, T, NB], BF16) for u in range(2)]
        masked = sb("masked", [P, T, NB])
        run = sb("run", [P, NB])
        base = sb("base", [P, NB])
        cnt = [sb(f"cnt{k}", [P, NB]) for k in range(3)]
        cnt_i = sb("cnt_i", [P, NB], I32)
        same = sb("same", [P, T, T])
        same8 = sb("same8", [P, T])
        rank8 = sb("rank8", [P, T])
        pos = [sb(f"pos{j}", [P, T], I32) for j in range(S)]
        gidx = [sb(f"gidx{j}", [P, T], I32) for j in range(S)]
        in_t = sb("in_t", [P, T * D])
        hid_t = sb("hid_t", [P, T * D])
        f_s = sb("f_s", [P, T, D])
        iota_i = f_s.rearrange("p t d -> p (t d)")[:, 0:2 * P].bitcast(I32)
        rest = sb("rest", [P, T * D])
        q_rows = [tmp_space[:, u * 4 * TQ * W:(u + 1) * 4 * TQ * W].rearrange("p (q t w) -> p q t w", q=4, t=TQ)
                  for u in range(2)]
        q_num_i = sb("q_num_i", [P, QC], I32)
        q_num = sb("q_num", [P, QC])
        q_cmp = sb("q_cmp", [P, QC, NB])
        q_blk = sb("q_blk", [P, QC])
        q_blk_i = sb("q_blk_i", [P, QC], I32)
        q_row = sb("q_row", [1, QC * P], I32)
        stat = [sb(f"stat{k}", [P, NB]) for k in range(2)]
        eps = sb("eps", [P, 1])
        wts = {k: sb(f"w_{k}", list(a.shape)) for k, a in w.items()}
        ends = [sb(f"ends{k}", [P, NGC * P]) for k in range(2)]
        col = sb("col", [P, 1])
        diag = sb("diag", [P, P])
        group_ends = [sb(f"group_ends{k}", [P, NGC * P]) for k in range(2)]
        base_i = sb("base_i", [P, NGC * P], I32)
        local_i = sb("local_i", [P, 1], I32)
        shifted = spaces[0][:, 0:NT].bitcast(I32)
        below = spaces[0][:, NT:2 * NT]
        rel_t = spaces[0][:, 2 * NT:2 * NT + NC * P // 2].bitcast(BF16).rearrange("p (c q) -> p c q", q=P)
        assert 2 * NT + NC * P // 2 <= spaces[0].shape[1]

        ps_t = pb("ps_t", [P, T * D])
        ps_h = pb("ps_h", [P, T * D])
        ps_f = pb("ps_f", [P, T * D])
        ps_x = pb("ps_x", [P, T * D])
        ps_rank = pb("ps_rank", [P, 512])
        ps_cnt = pb("ps_cnt", [P, 512])
        ps_agg = [pb(f"ps_agg{u}", [P, 512]) for u in range(2)]
        ps_win = [ps_agg, [ps_t, ps_h]]
        ps_all = [ps_agg[0], ps_agg[1], ps_t, ps_h, ps_f, ps_x, ps_rank, ps_cnt]

        def count_of(i, j, back=0):
            return i * S + (S + 1 + j - back)

        def seed(e, *sems, n=S):
            for s in sems:
                e.sem_inc(s, n)

        def stepper(e, s, n=0):
            n = [n]

            def step(ins):
                ins.then_inc(s, 1)
                n[0] += 1
                e.wait_ge(s, n[0])
            return step

        def by_locality(e, local, other):
            flag = e.value_load(local_i[0:1, 0:1], min_val=0, max_val=1)
            with e.If(flag > 0):
                local()
            with e.Else():
                other()

        def counting(layer, hi):
            c_oh, c_mm = shared_sem2("c_oh"), shared_sem2("c_mm")
            c_zero, c_tot, c_d = (shared_sem(f"c_{k}") for k in ("zero", "tot", "d"))
            c_dma, c_dma2 = (sem(f"c{layer}_{k}") for k in ("dma", "dma2"))

            def vector(e):
                with e.Fori(0, NG // 2) as i:
                    for u in range(2):
                        e.wait_ge(c_mm[u], i + 1)
                        e.tensor_tensor(
                            onehot[u][:, :, :],
                            hi[:, bass.ds(i * (2 * T) + u * T, T)].unsqueeze(2).broadcast_to([P, T, NB]),
                            iota[:, None, 0:NB].broadcast_to([P, T, NB]), ALU.is_equal).then_inc(c_oh[u], 1)
                e.wait_ge(c_tot, 1)
                step = stepper(e, c_d)
                step(e.tensor_reduce(cnt[0][:, :], ps_cnt[:, 0:HALF].rearrange("p (t b) -> p b t", b=NB),
                                     AX.X, ALU.add))
                step(e.tensor_scalar(cnt[0][:, :], cnt[0][:, :], float(ROWS_Q - 1), None, ALU.add))
                step(e.tensor_copy(cnt_i[:, :], cnt[0][:, :]))
                step(e.tensor_scalar(cnt_i[:, :], cnt_i[:, :], ROWS_Q.bit_length() - 1, None,
                                     ALU.logical_shift_right))
                step(e.tensor_copy(cnt[0][:, :], cnt_i[:, :]))
                a, b = cnt[1], cnt[2]
                step(e.tensor_copy(a[:, :], cnt[0][:, :]))
                k = 1
                while k < NB:
                    step(e.tensor_copy(b[:, 0:k], a[:, 0:k]))
                    step(e.tensor_tensor(b[:, k:NB], a[:, k:NB], a[:, 0:NB - k], ALU.add))
                    a, b = b, a
                    k *= 2
                step(e.tensor_tensor(
                    q_cmp[:, :, :], a[:, None, :].broadcast_to([P, QC, NB]),
                    q_num[:, :].unsqueeze(2).broadcast_to([P, QC, NB]), ALU.is_le))
                step(e.tensor_reduce(q_blk[:, :], q_cmp[:, :, :], AX.X, ALU.add))
                step(e.tensor_copy(q_blk_i[:, :], q_blk[:, :]))
                step(e.tensor_tensor(b[:, :], a[:, :], cnt[0][:, :], ALU.subtract))
                step(e.tensor_scalar(run[:, :], b[:, :], float(ROWS_Q), None, ALU.mult))

            n_steps = 6 + 2 * (NB - 1).bit_length() + 5

            def tensor(e):
                seed(e, *c_mm, n=1)
                e.matmul(ps_cnt[:, 0:HALF], ones[:, :], zeros[:, :], start=True, stop=False).then_inc(c_zero, 1)
                with e.Fori(0, NG // 2) as i:
                    for u in range(2):
                        e.wait_ge(c_oh[u], i + 1)
                        for h in range(2):
                            last = e.matmul(ps_cnt[:, 0:HALF], ones[:, :],
                                            onehot[u][:, h * (T // 2):(h + 1) * (T // 2), :].rearrange("p t b -> p (t b)"),
                                            start=False, stop=False)
                        last.then_inc(c_mm[u], 1)
                e.matmul(ps_cnt[:, 0:HALF], ones[:, :], zeros[:, :], start=False, stop=True).then_inc(c_tot, 1)

            def scalar(e):
                e.wait_ge(c_d, n_steps)
                with nc.allow_non_contiguous_dma(reason="a few hundred words"):
                    e.dma_start(q_block_row[0, :].rearrange("(c p) -> p c", p=P), q_blk_i[:, :]).then_inc(c_dma, 16)
                e.wait_ge(c_dma, 16)
                e.dma_start(q_row[:, :], q_block_row).then_inc(c_dma2, 16)
                e.wait_ge(c_dma2, 16)

            return vector, tensor, scalar

        s_const, s_in, s_x, s_zero, s_fill, s_d, s_pool = (
            sem(f"s_{k}") for k in ("const", "in", "x", "zero", "fill", "d", "pool"))
        w_t, w_ev, w_f, w_b, w_add, w_hi, w_r1, w_mid, w_lo = (
            sem(f"wxh_{k}") for k in ("t", "ev", "f", "b", "add", "hi", "r1", "mid", "lo"))
        w_out = sem2("wxh_out")
        wxh_f = [t.rearrange("p (t d) -> p t d", d=D) for t in (hid_t[:, :], rest[:, :])]
        g_t, g_bc, r_t, r_ev, r_out = (sem(k) for k in ("ends_t", "ends_bc", "rel_t_", "rel_ev", "rel_out"))
        fill = sorted_rows.rearrange("(c p r) w -> c p (r w)", p=P, r=FR)
        fill_from = agg[:, :, :].rearrange("p b d -> p (b d)")[:, 0:FR * W]
        GN = NBP // T
        KEYS = 3 + 9
        ENDS = KEYS + 4
        REL = ENDS + 2 * NGC * 3 + 7

        def set_up(count):
            c_vector, c_tensor, c_scalar = count
            with nc.Block() as block:
                @block.gpsimd
                def _(e):
                    e.iota(iota_i, pattern=[[1, 2 * P]], base=0, channel_multiplier=0).then_inc(s_pool, 1)
                    e.iota(node_iota_i[:, :], pattern=[[P, 2]], base=0, channel_multiplier=1).then_inc(s_pool, 1)
                    e.iota(q_num_i[:, :], pattern=[[P, QC]], base=0, channel_multiplier=1).then_inc(s_pool, 1)
                    for t, v in ((ident, 0.0), (ident_b, 0.0), (ones, 1.0), (ones_f, 1.0), (zeros, 0.0),
                                 (eps, 1e-5), (local_i, 0), (rel, 0.0), (ends[0], 0.0), (ends[1], 0.0)):
                        e.memset(t[:, :], v).then_inc(s_pool, 1)
                    e.memset(before8[:, :, :], 1.0).then_inc(s_pool, 1)
                    e.wait_ge(s_pool, 14)
                    for t in (ident, ident_b):
                        e.affine_select(out=t[:, :], in_=t[:, :], compare_op=ALU.not_equal, fill=1.0,
                                        base=0, pattern=[[-1, P]], channel_multiplier=1).then_inc(s_const, 1)
                    e.affine_select(out=tri[:, :], in_=ones[:, :], compare_op=ALU.is_gt, fill=0.0,
                                    base=0, pattern=[[1, P]], channel_multiplier=-1).then_inc(s_const, 1)
                    e.affine_select(out=before8[:, :, :], in_=before8[:, :, :], compare_op=ALU.is_gt, fill=0.0,
                                    base=0, pattern=[[1, T], [-1, T]], channel_multiplier=0).then_inc(s_const, 1)
                    r = wxh_rows.rearrange("(b p) d -> p b d", p=P)
                    for g in range(GN):
                        e.wait_ge(w_add, g + 1)
                        e.dma_start(r[:, g * T:(g + 1) * T, :], wxh_f[g % 2]).then_inc(w_out[g % 2], 16)
                    for k in range(2):
                        e.wait_ge(w_out[k], 16 * ((GN + 1 - k) // 2))

                @block.sync
                def _(e):
                    for t, a in ((src_i, src), (dst_i, dst), (ew_s, ew)):
                        e.dma_start(t[:, :], a).then_inc(s_in, 16)
                    e.dma_start(xs[:, :, :], x.rearrange("(b p) d -> p b d", p=P)).then_inc(s_x, 16)
                    e.wait_ge(s_zero, 1)
                    with e.Fori(0, FILL) as c:
                        e.dma_start(fill[bass.ds(c, 1), :, :].rearrange("c p n -> (c p) n"), fill_from).then_inc(s_fill, 16)
                    e.wait_ge(s_fill, 16 * FILL)

                @block.scalar
                def _(e):
                    for k, a in w.items():
                        e.dma_start(wts[k][:, :], a).then_inc(w_b, 16)
                    for c in range(NC):
                        e.wait_ge(r_t, c + 1)
                        e.copy(rel_t[:, c, :], ps_x[:, 0:P // 2].bitcast(BF16)).then_inc(r_ev, 1)
                    e.wait_ge(r_ev, NC)
                    e.dma_start(rel_rows.rearrange("(c t) p -> t c p", t=P), rel_t).then_inc(r_out, 16)
                    for g in range(GN):
                        e.wait_ge(w_t, g + 1)
                        e.wait_ge(w_f, g)
                        e.copy(in_t[:, :], ps_t[:, :]).then_inc(w_ev, 1)
                        for h in ((g - 1,) if g else ()) + ((g,) if g == GN - 1 else ()):
                            e.wait_ge(w_add, h + 1)
                            e.copy(wxh[:, h * T:(h + 1) * T, 0, :], wxh_f[h % 2]).then_inc(w_hi, 1)
                            e.wait_ge(w_r1, h + 1)
                            e.copy(wxh[:, h * T:(h + 1) * T, 1, :], f_s[:, :, :]).then_inc(w_mid, 1)
                    c_scalar(e)
                    e.wait_ge(r_out, 16)

                @block.tensor
                def _(e):
                    e.wait_ge(s_const, 4)
                    e.wait_ge(s_x, 16)
                    e.wait_ge(w_b, 16 * len(w))
                    at = ENDS
                    for k in range(2):
                        for c in range(NGC):
                            e.wait_ge(s_d, at)
                            e.transpose(ps_h[:, 0:P], ends[k][:, c * P:(c + 1) * P], ident[:, :]).then_inc(g_t, 1)
                            e.wait_ge(s_d, at + 2)
                            e.matmul(ps_h[:, P:2 * P], ones_f[:, :], diag[:, :], start=True, stop=True).then_inc(g_bc, 1)
                            at += 3
                    e.wait_ge(s_d, REL)
                    for c in range(NC):
                        e.wait_ge(r_ev, c)
                        e.transpose(ps_x[:, 0:P // 2].bitcast(BF16), rel[:, c * P:(c + 1) * P],
                                    ident_b[:, :]).then_inc(r_t, 1)
                    for g in range(GN):
                        e.wait_ge(w_ev, g)
                        for k in range(T // 2):
                            pair = xs[:, g * T + 2 * k:g * T + 2 * k + 2, :].rearrange("p b d -> p (b d)")
                            last = e.transpose(ps_t[:, k * P:(k + 1) * P], pair, ident[:, :])
                        last.then_inc(w_t, 1)
                        e.wait_ge(w_ev, g + 1)
                        e.wait_ge(w_add, g)
                        for k in range(T // 2):
                            last = e.matmul(ps_f[:, k * P:(k + 1) * P], in_t[:, k * P:(k + 1) * P],
                                            wts["wl"][:, :], start=True, stop=True)
                        last.then_inc(w_f, 1)
                    c_tensor(e)

                @block.vector
                def _(e):
                    e.memset(agg[:, :, :], 0.0).then_inc(s_zero, 1)
                    step = stepper(e, s_d)
                    e.wait_ge(s_pool, 14)
                    step(e.tensor_copy(iota[:, :], iota_i))
                    step(e.tensor_copy(q_num[:, :], q_num_i[:, :]))
                    step(e.tensor_copy(node_iota[:, :], node_iota_i[:, :]))
                    e.wait_ge(s_in, 48)
                    for a, hi, lo in ((src_i, hi_s, lo_s), (dst_i, hi_d, lo_d)):
                        step(e.tensor_scalar(shifted, a[:, :], 7, None, ALU.logical_shift_right))
                        step(e.tensor_copy(hi[:, :], shifted))
                        step(e.tensor_scalar(shifted, a[:, :], P - 1, None, ALU.bitwise_and))
                        step(e.tensor_copy(lo[:, :], shifted))
                    step(e.tensor_scalar(far[:, :], hi_s[:, :], float(NB), FAR, ALU.is_ge, ALU.mult))
                    grouped = lambda a: a.rearrange("p (g t) -> p g t", t=T)
                    step(e.tensor_reduce(ends[0][:, 0:NG], grouped(hi_d[:, :]), AX.X, ALU.min))
                    step(e.tensor_scalar(below, hi_d[:, :], float(NB), None, ALU.is_lt))
                    step(e.tensor_tensor(below, below, hi_d[:, :], ALU.mult))
                    step(e.tensor_reduce(ends[1][:, 0:NG], grouped(below), AX.X, ALU.max))
                    n = 0
                    for k, op in enumerate((ALU.min, ALU.max)):
                        for c in range(NGC):
                            n += 1
                            e.wait_ge(g_t, n)
                            step(e.tensor_reduce(col[:, :], ps_h[:, 0:P], AX.X, op))
                            step(e.tensor_scalar(diag[:, :], ident[:, :], col[:, 0:1], None, ALU.mult))
                            e.wait_ge(g_bc, n)
                            step(e.tensor_copy(group_ends[k][:, c * P:(c + 1) * P], ps_h[:, P:2 * P]))
                    first, last = (t[:, 0:NG] for t in group_ends)
                    spread = ends[0][:, 0:NG]
                    step(e.tensor_tensor(spread, last, first, ALU.subtract))
                    step(e.tensor_reduce(col[:, :], spread, AX.X, ALU.max))
                    step(e.tensor_scalar(local_i[:, :], col[:, :], 1.5, None, ALU.is_lt))
                    step(e.tensor_scalar(first, first, float(NB - 1), None, ALU.min))
                    step(e.tensor_copy(base_i[:, 0:NG], first))
                    step(e.tensor_tensor(grouped(below), grouped(hi_d[:, :]),
                                         first.unsqueeze(2).broadcast_to([P, NG, T]), ALU.subtract))
                    step(e.scalar_tensor_tensor(out=rel[:, 0:NT], in0=below, scalar=float(P), in1=lo_d[:, :],
                                                op0=ALU.mult, op1=ALU.add))
                    for g in range(GN):
                        blocks = slice(g * T, (g + 1) * T)
                        e.wait_ge(w_f, g + 1)
                        if g >= 2:
                            e.wait_ge(w_out[g % 2], 16 * (g // 2))
                        e.tensor_tensor(wxh_f[g % 2], ps_f[:, :].rearrange("p (t d) -> p t d", d=D),
                                        wts["bl"][:, None, :].broadcast_to([P, T, D]), ALU.add).then_inc(w_add, 1)
                        e.wait_ge(w_lo, g)
                        e.wait_ge(w_hi, g + 1)
                        e.tensor_tensor(f_s[:, :, :], wxh_f[g % 2], wxh[:, blocks, 0, :], ALU.subtract).then_inc(w_r1, 1)
                        e.wait_ge(w_mid, g + 1)
                        e.tensor_tensor(wxh[:, blocks, 2, :], f_s[:, :, :], wxh[:, blocks, 1, :],
                                        ALU.subtract).then_inc(w_lo, 1)
                    c_vector(e)

        def count_again(layer, hi):
            vector, tensor, scalar = counting(layer, hi)
            with nc.Block() as block:
                block.vector(unless_local(vector))
                block.tensor(unless_local(tensor))
                block.scalar(unless_local(scalar))

        def unless_local(body):
            def run_(e):
                flag = e.value_load(local_i[0:1, 0:1], min_val=0, max_val=1)
                with e.If(flag < 1):
                    body(e)
            return run_

        def messages(layer, hi, lo, idx, table):
            rows_, gathered_, rbf_ = (S, T, W), (S, T, D), (S, T * D)
            found = carve(layer, rows_, gathered_, rbf_)
            rows, gathered, rbf_s = found[0:S], found[S:2 * S], found[2 * S:3 * S]
            xg, sc, ld, rl = ([sem(f"m{layer}_{k}_{j}") for j in range(S)] if k in ("xg", "sc") or layer == 0 else None
                              for k in ("xg", "sc", "ld", "rl"))
            gi, m, lo_w, oh, rk, bs, rn, ww, pr, pr2, c1, c2, c3, po, tr, ev, h1, si, f2, f1, wi, xw = (
                shared_sem(f"m_{k}") for k in (
                    "gi", "m", "lo", "oh", "rk", "bs", "rn", "ww", "pr", "pr2", "c1", "c2", "c3", "po",
                    "tr", "ev", "h1", "si", "f2", "f1", "wi", "xw"))
            passes = NG // S
            tiles = lambda i, j: bass.ds(i * (S * T) + j * T, T)

            def sync(e, local):
                r = rbf.rearrange("(g p t) k -> g p (t k)", p=P, t=T)
                q = rel_rows[0:NT, :].rearrange("(g t) p -> g (t p)", t=T)
                with e.Fori(0, passes) as i:
                    for j in range(S):
                        e.wait_ge(tr, count_of(i, j, S))
                        e.dma_start(rbf_s[j], r[bass.ds(i * S + j, 1), :, :].rearrange("g p n -> (g p) n")
                                    ).then_inc(ld[j], 16)
                        if local:
                            e.wait_ge(wi, count_of(i, j, 2))
                            e.dma_start(rel_bc[j % 2][:, :], q[bass.ds(i * S + j, 1), :].broadcast_to([P, T * P])
                                        ).then_inc(rl[j], 16)

            def scalar(e):
                with e.Fori(0, passes) as i:
                    for j in range(S):
                        if layer == 0:
                            e.wait_ge(h1, count_of(i, j, 1))
                            e.wait_ge(tr, count_of(i, j))
                            e.copy(in_t[:, :], ps_t[:, :]).then_inc(ev, 1)
                        e.wait_ge(sc[j], i * (16 * T) + 16 * T)
                        e.copy(rows[j][:, :, D], lo[:, tiles(i, j)]).then_inc(lo_w, 1)
                        if layer == 0:
                            e.wait_ge(f2, count_of(i, j, 1))
                            e.wait_ge(h1, count_of(i, j))
                            e.activation(hid_t[:, :], ps_h[:, :], ACT.Silu, bias=wts["bf1"][:, 0:1]).then_inc(si, 1)

            def tensor(e, local):
                with e.Fori(0, passes) as i:
                    for j in range(S):
                        if layer == 0:
                            e.wait_ge(ld[j], i * 16 + 16)
                            e.wait_ge(ev, count_of(i, j, 1))
                            for t in range(T // 2):
                                last = e.transpose(ps_t[:, t * P:(t + 1) * P],
                                                   rbf_s[j][:, t * P:(t + 1) * P], ident[:, :])
                            last.then_inc(tr, 1)
                        e.wait_ge(rn, count_of(i, j, 1))
                        e.wait_ge(oh, count_of(i, j))
                        for t in range(T):
                            e.matmul(ps_rank[:, 0:NB], tri[:, :], onehot[j % 2][:, t, :],
                                     start=(t == 0), stop=(t == T - 1))
                        for t in range(T):
                            last = e.matmul(ps_cnt[:, 0:NB], ones[:, :], onehot[j % 2][:, t, :],
                                            start=(t == 0), stop=(t == T - 1))
                        last.then_inc(rk, 1)
                        if layer:
                            continue
                        e.wait_ge(si, count_of(i, j, 1))
                        e.wait_ge(ev, count_of(i, j))
                        e.matmul(ps_h[:, :], wts["wf1"][:, :], in_t[:, :], start=True, stop=True).then_inc(h1, 1)
                        if local:
                            b = e.value_load(base_i[0:1, bass.ds(i * S + j, 1)], min_val=0, max_val=NB - 1)
                            e.wait_ge(m, count_of(i, j, 1))
                            e.wait_ge(wi, count_of(i, j))
                            for t in range(T):
                                for h in range(2):
                                    for c in range(PARTS):
                                        last = e.matmul(
                                            ps_x[:, t * D:(t + 1) * D], window_t[:, h, t * P:(t + 1) * P],
                                            wxh[:, bass.ds(b + h, 1), c, :].rearrange("p b d -> p (b d)"),
                                            start=(h == 0 and c == 0), stop=(h == 1 and c == PARTS - 1))
                            last.then_inc(xw, 1)
                        e.wait_ge(f1, count_of(i, j, 1))
                        e.wait_ge(si, count_of(i, j))
                        for t in range(T // 2):
                            last = e.matmul(ps_f[:, t * P:(t + 1) * P], hid_t[:, t * P:(t + 1) * P],
                                            wts["wf2"][:, :], start=True, stop=True)
                        last.then_inc(f2, 1)

            def vector(e, local):
                with e.Fori(0, passes) as i:
                    for j in range(S):
                        at = tiles(i, j)
                        if not local:
                            e.wait_ge(m, count_of(i, j, S))
                            e.tensor_copy(gidx[j][:, :], idx[:, at]).then_inc(gi, 1)
                        e.wait_ge(rk, count_of(i, j, 2))
                        e.wait_ge(ww, count_of(i, j, 2))
                        e.tensor_tensor(onehot[j % 2][:, :, :], hi[:, at].unsqueeze(2).broadcast_to([P, T, NB]),
                                        iota[:, None, 0:NB].broadcast_to([P, T, NB]), ALU.is_equal).then_inc(oh, 1)
                        if local:
                            e.wait_ge(rl[j], i * 16 + 16)
                            e.wait_ge(xw, count_of(i, j, 1))
                            for h in range(2):
                                last = e.tensor_scalar(window_t[:, h, :], rel_bc[j % 2][:, :],
                                                       node_iota[:, h:h + 1], None, ALU.is_equal)
                            last.then_inc(wi, 1)
                        e.wait_ge(c3, count_of(i, j, 1))
                        e.tensor_tensor(same[:, :, :], hi[:, at].unsqueeze(2).broadcast_to([P, T, T]),
                                        hi[:, at].unsqueeze(1).broadcast_to([P, T, T]), ALU.is_equal).then_inc(c1, 1)
                        e.wait_ge(c1, count_of(i, j))
                        e.tensor_tensor(same[:, :, :], same[:, :, :], before8[:, :, :], ALU.mult).then_inc(c2, 1)
                        e.wait_ge(po, count_of(i, j, 1))
                        e.wait_ge(c2, count_of(i, j))
                        e.tensor_reduce(same8[:, :], same[:, :, :], AX.X, ALU.add).then_inc(c3, 1)
                        e.wait_ge(ww, count_of(i, j, 1))
                        e.wait_ge(rn, count_of(i, j, 1))
                        e.wait_ge(rk, count_of(i, j))
                        e.tensor_tensor(base[:, :], run[:, :], ps_rank[:, 0:NB], ALU.add).then_inc(bs, 1)
                        e.wait_ge(bs, count_of(i, j))
                        e.tensor_tensor(run[:, :], run[:, :], ps_cnt[:, 0:NB], ALU.add).then_inc(rn, 1)
                        e.wait_ge(pr, count_of(i, j, 1))
                        e.tensor_tensor(masked[:, :, :], onehot[j % 2][:, :, :],
                                        base[:, None, :].broadcast_to([P, T, NB]), ALU.mult).then_inc(ww, 1)
                        e.wait_ge(c3, count_of(i, j))
                        e.wait_ge(ww, count_of(i, j))
                        e.tensor_reduce(rank8[:, :], masked[:, :, :], AX.X, ALU.add).then_inc(pr, 1)
                        e.wait_ge(pr, count_of(i, j))
                        e.tensor_tensor(rank8[:, :], rank8[:, :], same8[:, :], ALU.add).then_inc(pr2, 1)
                        e.wait_ge(sc[j], i * (16 * T) + 16 * T)
                        e.wait_ge(pr2, count_of(i, j))
                        e.tensor_tensor(pos[j][:, :], rank8[:, :], far[:, at], ALU.add).then_inc(po, 1)
                        if layer == 0:
                            e.wait_ge(m, count_of(i, j, 1))
                            e.wait_ge(f2, count_of(i, j))
                            e.tensor_tensor(f_s[:, :, :], ps_f[:, :].rearrange("p (t d) -> p t d", d=D),
                                            wts["bf2"][:, None, :].broadcast_to([P, T, D]), ALU.add).then_inc(f1, 1)
                            e.wait_ge(f1, count_of(i, j))
                        if local:
                            e.wait_ge(xw, count_of(i, j))
                            rows_in = ps_x[:, :].rearrange("p (t d) -> p t d", d=D)
                        else:
                            e.wait_ge(xg[j], i * (16 * T) + 16 * T)
                            rows_in = gathered[j]
                        other = f_s[:, :, :] if layer == 0 else ew_s[:, at].unsqueeze(2).broadcast_to([P, T, D])
                        e.tensor_tensor(rows[j][:, :, 0:D], rows_in, other, ALU.mult).then_inc(m, 1)

            def gpsimd(e, local):
                def gather(j, i):
                    if local:
                        return
                    e.wait_ge(m, count_of(i, j, S))
                    e.wait_ge(gi, count_of(i, j))
                    e.sem_inc(s_go, 1)
                    for t in range(T):
                        e.indirect_dma_start(
                            out=gathered[j][:, t, :], out_offset=None, in_=table,
                            in_offset=bass.IndirectOffsetOnAxis(ap=gidx[j][:, t:t + 1], axis=0),
                            bounds_check=n_nodes - 1, oob_is_err=False).then_inc(xg[j], 16)

                def scatter(j, i):
                    e.wait_ge(m, count_of(i, j))
                    e.wait_ge(lo_w, count_of(i, j))
                    e.wait_ge(po, count_of(i, j))
                    e.sem_inc(s_go, 1)
                    for t in range(T):
                        e.indirect_dma_start(
                            out=sorted_rows, out_offset=bass.IndirectOffsetOnAxis(ap=pos[j][:, t:t + 1], axis=0),
                            in_=rows[j][:, t, :], in_offset=None,
                            bounds_check=NQ * ROWS_Q - 1, oob_is_err=False).then_inc(sc[j], 16)

                gather(0, 0)
                with e.Fori(0, passes - 1) as i:
                    for j in range(S):
                        gather((j + 1) % S, i + (j + 1) // S)
                        scatter(j, i)
                i = passes - 1
                for j in range(S):
                    if j + 1 < S:
                        gather(j + 1, i)
                    scatter(j, i)

            with nc.Block() as block:
                def part(seeds, body, takes_local=True):
                    def run_(e):
                        seed(e, *seeds)
                        if not takes_local:
                            return body(e) if layer == 0 else unless_local(body)(e)
                        if layer:
                            return unless_local(lambda e: body(e, False))(e)
                        by_locality(e, lambda: body(e, True), lambda: body(e, False))
                    return run_

                zero = layer == 0
                if zero:
                    block.sync(part((), sync))
                block.scalar(part((ev, si, lo_w), scalar, takes_local=False))
                block.tensor(part((rk, tr, h1, f2, xw), tensor))
                block.vector(part((gi, oh, wi, c1, c2, c3, bs, rn, ww, pr, pr2, po, f1, m), vector))

                @block.gpsimd
                def _(e):
                    for j in range(S):
                        e.memset(gathered[j], 0.0).then_inc(s_pad, 1)
                    e.wait_ge(s_pad, S * (layer + 1))
                    for j in range(S):
                        e.dma_start(seed_rows[j:j + 1, :], zeros[0:1, 0:16]).then_inc(sc[j], 16 * T)
                    for j in range(S):
                        e.wait_ge(sc[j], 16 * T)
                    part((), gpsimd)(e)

                    def all_scattered(e):
                        for j in range(S):
                            e.wait_ge(sc[j], 16 * T * (passes + 1))

                    def all_gathered(e):
                        for j in range(S):
                            e.wait_ge(xg[j], 16 * T * passes)
                    (all_scattered if zero else unless_local(all_scattered))(e)
                    unless_local(all_gathered)(e)

        def window_sums():
            found = carve(1, (S, T, D), (2, T, D), (2, T, D // 2), (2, T, D // 2), (2, T, D // 2))
            gathered, msg, parts = found[0:S], found[S:S + 2], found[S + 2:]
            parts = [[parts[2 * c + k].bitcast(BF16) for c in range(PARTS)] for k in range(2)]
            xg = [sem(f"l1_xg_{j}") for j in range(S)]
            gi, m, wi, mm, ac, p1, r1, p2, p3 = (
                sem(f"l1_{k}") for k in ("gi", "m", "wi", "mm", "ac", "p1", "r1", "p2", "p3"))
            passes = NG // S
            tiles = lambda i, j: bass.ds(i * (S * T) + j * T, T)

            def vector(e):
                def indices(i, j):
                    e.wait_ge(m, count_of(i, j, S))
                    e.tensor_copy(gidx[j][:, :], src_i[:, tiles(i, j)]).then_inc(gi, 1)

                def group(i, j):
                    at = tiles(i, j)
                    b = e.value_load(base_i[0:1, bass.ds(i * S + j, 1)], min_val=0, max_val=NB - 1)
                    e.wait_ge(xg[j], i * (16 * T) + 16 * T)
                    e.wait_ge(p1, count_of(i, j, 2))
                    e.wait_ge(r1, count_of(i, j, 2))
                    e.tensor_tensor(msg[j % 2], gathered[j],
                                    ew_s[:, at].unsqueeze(2).broadcast_to([P, T, D]), ALU.mult).then_inc(m, 1)
                    e.wait_ge(mm, count_of(i, j, 1))
                    e.tensor_tensor(window_e, rel[:, at].unsqueeze(2).broadcast_to([P, T, 2 * P]),
                                    iota[:, None, :].broadcast_to([P, T, 2 * P]), ALU.is_equal).then_inc(wi, 1)
                    e.wait_ge(p1, count_of(i, j))
                    e.wait_ge(p3, count_of(i, j, 1))
                    e.tensor_tensor(rest[:, :].rearrange("p (t d) -> p t d", d=D), msg[j % 2], parts[j % 2][0],
                                    ALU.subtract).then_inc(r1, 1)
                    e.wait_ge(p2, count_of(i, j))
                    e.tensor_tensor(parts[j % 2][2], rest[:, :].rearrange("p (t d) -> p t d", d=D), parts[j % 2][1],
                                    ALU.subtract).then_inc(p3, 1)
                    e.wait_ge(mm, count_of(i, j))
                    e.wait_ge(ac, count_of(i, j, 1))
                    for h in range(2):
                        to = agg[:, bass.ds(b + h, 1), :].rearrange("p b d -> p (b d)")
                        last = e.tensor_tensor(to, to, ps_win[j % 2][h][:, 0:D], ALU.add)
                    last.then_inc(ac, 1)

                for j in range(S):
                    indices(0, j)
                with e.Fori(0, passes - 1) as i:
                    for j in range(S):
                        group(i, j)
                        indices(i + 1, j)
                for j in range(S):
                    group(passes - 1, j)

            def tensor(e):
                with e.Fori(0, passes) as i:
                    for j in range(S):
                        e.wait_ge(ac, count_of(i, j, 2))
                        e.wait_ge(wi, count_of(i, j))
                        e.wait_ge(p3, count_of(i, j))
                        for h in range(2):
                            for t in range(T):
                                for c in range(PARTS):
                                    last = e.matmul(ps_win[j % 2][h][:, 0:D], window_e[:, t, h * P:(h + 1) * P],
                                                    parts[j % 2][c][:, t, :], start=(t == 0 and c == 0),
                                                    stop=(t == T - 1 and c == PARTS - 1))
                        last.then_inc(mm, 1)

            def scalar(e):
                with e.Fori(0, passes) as i:
                    for j in range(S):
                        e.wait_ge(mm, count_of(i, j, 2))
                        e.wait_ge(m, count_of(i, j))
                        e.copy(parts[j % 2][0], msg[j % 2]).then_inc(p1, 1)
                        e.wait_ge(r1, count_of(i, j))
                        e.copy(parts[j % 2][1], rest[:, :].rearrange("p (t d) -> p t d", d=D)).then_inc(p2, 1)

            def gpsimd(e):
                for j in range(S):
                    e.memset(gathered[j], 0.0).then_inc(s_pad, 1)
                e.wait_ge(s_pad, 2 * S)
                with e.Fori(0, passes) as i:
                    for j in range(S):
                        e.wait_ge(m, count_of(i, j, S))
                        e.wait_ge(gi, count_of(i, j))
                        e.sem_inc(s_go, 1)
                        for t in range(T):
                            e.indirect_dma_start(
                                out=gathered[j][:, t, :], out_offset=None, in_=x1_rows,
                                in_offset=bass.IndirectOffsetOnAxis(ap=gidx[j][:, t:t + 1], axis=0),
                                bounds_check=n_nodes - 1, oob_is_err=False).then_inc(xg[j], 16)
                for j in range(S):
                    e.wait_ge(xg[j], 16 * T * passes)

            with nc.Block() as block:
                def part(seeds, body):
                    def run_(e):
                        seed(e, *seeds)
                        flag = e.value_load(local_i[0:1, 0:1], min_val=0, max_val=1)
                        with e.If(flag > 0):
                            body(e)
                    return run_
                block.vector(part((gi, m, wi, ac, r1, p3), vector))
                block.scalar(part((p1, p2), scalar))
                block.tensor(part((mm,), tensor))
                block.gpsimd(part((), gpsimd))

        def reduce_rows(layer):
            n_parts = 4 * TQ * D // 2
            found = carve(layer, *[(2, n_parts)] * PARTS, (2, 2 * n_parts), (4, TQ * P // 2))
            parts = [[found[2 * c + u].bitcast(BF16).rearrange("p (n d) -> p n d", d=D) for c in range(PARTS)]
                     for u in range(2)]
            left = [found[2 * PARTS + u].rearrange("p (n d) -> p n d", d=D) for u in range(2)]
            q_onehot = [a.bitcast(BF16).rearrange("p (t n) -> p t n", t=TQ) for a in found[2 * PARTS + 2:]]
            data = [q_rows[u].rearrange("p q t w -> p (q t) w")[:, :, 0:D] for u in range(2)]
            ld = sem2(f"r{layer}_ld")
            oh, mm, ac, p1, p2, p3, r1 = (shared_sem(f"r_{k}") for k in ("oh", "mm", "ac", "p1", "p2", "p3", "r1"))
            only = (lambda body: body) if layer == 0 else unless_local
            passes = NQ // 8

            def done(i, q, back=0):
                return i * 8 + (9 + q - back)

            def done2(i, u, back=0):
                return i * 2 + (3 + u - back)

            with nc.Block() as block:
                @block.sync
                @only
                def _(e):
                    r = sorted_rows.rearrange("(c q p t) w -> c p q (t w)", q=4, p=P, t=TQ)
                    with e.Fori(0, passes) as i:
                        for u in range(2):
                            e.wait_ge(oh, done(i, 4 * u + 3, 8))
                            e.dma_start(q_rows[u].rearrange("p q t w -> p q (t w)"),
                                        r[bass.ds(i * 2 + u, 1), :, :, :].rearrange("c p q n -> (c p) q n")).then_inc(ld[u], 16)
                    for u in range(2):
                        e.wait_ge(ld[u], 16 * passes)

                @block.scalar
                @only
                def _(e):
                    seed(e, p1, p2, n=2)
                    with e.Fori(0, passes) as i:
                        for u in range(2):
                            e.wait_ge(ld[u], i * 16 + 16)
                            e.wait_ge(mm, done(i, 4 * u + 3, 8))
                            e.copy(parts[u][0], data[u]).then_inc(p1, 1)
                            e.wait_ge(r1, done2(i, u))
                            e.copy(parts[u][1], left[u]).then_inc(p2, 1)

                @block.gpsimd
                @only
                def _(e):
                    seed(e, r1, n=2)
                    with e.Fori(0, passes) as i:
                        for u in range(2):
                            e.wait_ge(p3, done2(i, u, 2))
                            e.wait_ge(p1, done2(i, u))
                            e.tensor_tensor(left[u], data[u], parts[u][0], ALU.subtract).then_inc(r1, 1)

                @block.tensor
                @only
                def _(e):
                    seed(e, mm, n=8)
                    with e.Fori(0, passes) as i:
                        for q in range(8):
                            if q % 4 == 0:
                                e.wait_ge(p3, done2(i, q // 4))
                            e.wait_ge(ac, done(i, q, 8))
                            e.wait_ge(oh, done(i, q))
                            for t in range(TQ):
                                for c in range(PARTS):
                                    last = e.matmul(ps_all[q][:, 0:D], q_onehot[q % 4][:, t, :],
                                                    parts[q // 4][c][:, q % 4 * TQ + t, :],
                                                    start=(t == 0 and c == 0), stop=(t == TQ - 1 and c == PARTS - 1))
                            last.then_inc(mm, 1)

                @block.vector
                @only
                def _(e):
                    seed(e, oh, ac, n=8)
                    seed(e, p3, n=2)

                    def rows_onehot(i, q):
                        if q % 4 == 0:
                            e.wait_ge(ld[q // 4], i * 16 + 16)
                        e.wait_ge(mm, done(i, q, 4))
                        for t in range(TQ):
                            last = e.tensor_scalar(q_onehot[q % 4][:, t, :], iota[:, 0:P],
                                                   q_rows[q // 4][:, q % 4, t, D:D + 1], None, ALU.is_equal)
                        last.then_inc(oh, 1)

                    def last_part(i, u):
                        e.wait_ge(p2, done2(i, u))
                        e.tensor_tensor(parts[u][2], left[u], parts[u][1], ALU.subtract).then_inc(p3, 1)

                    def add(i, q, b):
                        e.wait_ge(mm, done(i, q))
                        e.wait_ge(ac, done(i, q, 1))
                        to = agg[:, bass.ds(b, 1), :].rearrange("p b d -> p (b d)")
                        e.tensor_tensor(to, to, ps_all[q][:, 0:D], ALU.add).then_inc(ac, 1)

                    AHEAD = 3
                    with e.Fori(0, passes) as i:
                        held = []
                        for q in range(8 + AHEAD):
                            if q < 8:
                                rows_onehot(i, q)
                            if q % 4 == 0 and q < 8:
                                last_part(i, q // 4)
                                _, blocks = nc.values_load_multi_w_load_instructions(
                                    q_row[0:1, bass.ds(i * 8 + q, 4)], engines=[mybir.EngineType.DVE],
                                    min_val=0, max_val=NB)
                                held += list(blocks)
                            if q >= AHEAD:
                                add(i, q - AHEAD, held[q - AHEAD])

        def norm_steps(e, step, to, of, square, s_act, s_var, nth):
            bc = lambda a: a[:, :].unsqueeze(2).broadcast_to([P, NB, D])
            step(e.tensor_reduce(stat[0][:, :], of, AX.X, ALU.add))
            step(e.tensor_scalar(stat[0][:, :], stat[0][:, :], 1.0 / D, None, ALU.mult))
            step(e.tensor_tensor(to, of, bc(stat[0]), ALU.subtract))
            step(e.tensor_tensor(square, to, to, ALU.mult))
            step(e.tensor_reduce(stat[0][:, :], square, AX.X, ALU.add))
            e.sem_inc(s_var, 1)
            e.wait_ge(s_act, nth)
            step(e.reciprocal(stat[0][:, :], stat[1][:, :]))
            step(e.tensor_tensor(to, to, bc(stat[0]), ALU.mult))

        def root(e, s_act, s_var, nth):
            e.wait_ge(s_var, nth)
            e.activation(stat[1][:, :], stat[0][:, :], ACT.Sqrt, scale=1.0 / D, bias=eps[:, 0:1]).then_inc(s_act, 1)

        def node_update():
            d_, a_, v_, done, o_ = (sem(f"n0_{k}") for k in ("d", "a", "v", "done", "o"))
            A, X, X1, Y = (t[:, 0:NB, :] for t in (agg, xs, x1, tmp))
            bc = lambda a: a[:, None, :].broadcast_to([P, NB, D])
            with nc.Block() as block:
                @block.vector
                def _(e):
                    step = stepper(e, d_)
                    step(e.memset(x1[:, NB:NBP, :], 0.0))
                    step(e.tensor_tensor(A, A, X, ALU.add))
                    norm_steps(e, step, A, A, Y, a_, v_, 1)
                    step(e.tensor_tensor(A, A, bc(wts["gamma"]), ALU.mult))
                    step(e.tensor_tensor(A, A, bc(wts["beta"]), ALU.add))
                    step(e.tensor_tensor(A, A, X, ALU.add))
                    norm_steps(e, step, X1, A, Y, a_, v_, 2)
                    e.sem_inc(done, 1)
                    step(e.memset(agg[:, :, :], 0.0))

                @block.scalar
                def _(e):
                    root(e, a_, v_, 1)
                    root(e, a_, v_, 2)

                @block.sync
                def _(e):
                    e.wait_ge(done, 1)
                    e.dma_start(x1_rows.rearrange("(b p) d -> p b d", p=P), X1).then_inc(o_, 16)
                    e.wait_ge(o_, 16)

        def refill():
            f_ = sem("refill")
            with nc.Block() as block:
                @block.sync
                @unless_local
                def _(e):
                    with e.Fori(0, FILL) as c:
                        e.dma_start(fill[bass.ds(c, 1), :, :].rearrange("c p n -> (c p) n"), fill_from).then_inc(f_, 16)
                    e.wait_ge(f_, 16 * FILL)

                @block.vector
                def _(e):
                    for s in shared.values():
                        e.sem_clear(s)

        def node_mlp():
            d_, a_, v_, add, t_, ev, h1, re, f2, f1, o_ = (
                sem(f"n1_{k}") for k in ("d", "a", "v", "add", "t", "ev", "h1", "re", "f2", "f1", "o"))
            A, X1, Y = (t[:, 0:NB, :] for t in (agg, x1, tmp))
            G = NBP // T
            with nc.Block() as block:
                @block.vector
                def _(e):
                    step = stepper(e, d_)
                    step(e.tensor_tensor(agg[:, :, :], agg[:, :, :], x1[:, :, :], ALU.add))
                    e.sem_inc(add, 1)
                    for g in range(G):
                        e.wait_ge(f2, g + 1)
                        to = tmp[:, g * T:(g + 1) * T, :]
                        step(e.tensor_tensor(to, ps_f[:, :].rearrange("p (t d) -> p t d", d=D),
                                             x1[:, g * T:(g + 1) * T, :], ALU.add))
                        e.sem_inc(f1, 1)
                        step(e.tensor_tensor(to, to, wts["b2"][:, None, :].broadcast_to([P, T, D]), ALU.add))
                    norm_steps(e, step, Y, Y, A, a_, v_, 1)
                    e.sem_inc(add, 1)

                @block.tensor
                def _(e):
                    e.wait_ge(add, 1)
                    for g in range(G):
                        e.wait_ge(ev, g)
                        for k in range(T // 2):
                            pair = agg[:, g * T + 2 * k:g * T + 2 * k + 2, :].rearrange("p b d -> p (b d)")
                            last = e.transpose(ps_t[:, k * P:(k + 1) * P], pair, ident[:, :])
                        last.then_inc(t_, 1)
                        e.wait_ge(re, g)
                        e.wait_ge(ev, g + 1)
                        e.matmul(ps_h[:, :], wts["w1"][:, :], in_t[:, :], start=True, stop=True).then_inc(h1, 1)
                        e.wait_ge(f1, g)
                        e.wait_ge(re, g + 1)
                        for k in range(T // 2):
                            last = e.matmul(ps_f[:, k * P:(k + 1) * P], hid_t[:, k * P:(k + 1) * P],
                                            wts["w2"][:, :], start=True, stop=True)
                        last.then_inc(f2, 1)

                @block.scalar
                def _(e):
                    for g in range(G):
                        e.wait_ge(h1, g)
                        e.wait_ge(t_, g + 1)
                        e.activation(in_t[:, :], ps_t[:, :], ACT.Copy).then_inc(ev, 1)
                        e.wait_ge(f2, g)
                        e.wait_ge(h1, g + 1)
                        e.activation(hid_t[:, :], ps_h[:, :], ACT.Relu, bias=wts["b1"][:, 0:1]).then_inc(re, 1)
                    root(e, a_, v_, 1)

                @block.sync
                def _(e):
                    e.wait_ge(add, 2)
                    e.dma_start(out.rearrange("(b p) d -> p b d", p=P), Y).then_inc(o_, 16)
                    e.wait_ge(o_, 16)

        s_pad = sem("s_pad")
        s_go = sem("s_go")
        set_up(counting(0, hi_s))
        messages(0, hi_s, lo_s, dst_i, wxh_rows)
        reduce_rows(0)
        node_update()
        window_sums()
        refill()
        count_again(1, hi_d)
        messages(1, hi_d, lo_d, src_i, x1_rows)
        reduce_rows(1)
        node_mlp()


def kernel(x, src, dst, edge_attr_64, edge_weight, L0_gnn_Wf1, L0_gnn_bf1, L0_gnn_Wf2, L0_gnn_bf2, L0_gnn_Wl,
           L0_gnn_bl, L0_gnn_gamma, L0_gnn_beta, L1_gnn_W1, L1_gnn_b1, L1_gnn_W2, L1_gnn_b2):
    import concourse.bacc as bacc
    import numpy as np
    from concourse.bass_utils import run_bass_kernel_spmd

    x, src, dst, rbf, ew = (np.asarray(a) for a in (x, src, dst, edge_attr_64, edge_weight))
    n_nodes, n_edges = x.shape[0], src.shape[0]
    NB, NBP, NG, NQ = sizes(n_nodes, n_edges)
    pad_node = (2 * NB) * P

    def edges(a, fill):
        a = np.concatenate([a, np.full(NG * T * P - n_edges, fill, a.dtype)])
        return np.ascontiguousarray(a.reshape(NG, P, T).transpose(1, 0, 2).reshape(P, NG * T))

    def twice(a):
        a = np.asarray(a)
        z = np.zeros_like(a)
        return np.ascontiguousarray(np.block([[a, z], [z, a]]))

    def column(a):
        return np.ascontiguousarray(np.concatenate([a, a]).reshape(P, 1))

    def spread(a):
        return np.ascontiguousarray(np.broadcast_to(np.asarray(a), (P, D)))

    w = {
        "wf1": twice(np.asarray(L0_gnn_Wf1).T), "wf2": twice(np.asarray(L0_gnn_Wf2).T),
        "wl": twice(np.asarray(L0_gnn_Wl).T), "w1": twice(L1_gnn_W1), "w2": twice(L1_gnn_W2),
        "bf1": column(L0_gnn_bf1), "b1": column(L1_gnn_b1),
        "bf2": spread(L0_gnn_bf2), "bl": spread(L0_gnn_bl), "gamma": spread(L0_gnn_gamma),
        "beta": spread(L0_gnn_beta), "b2": spread(L1_gnn_b2),
    }
    arrays = {
        "x": np.concatenate([x, np.zeros((NBP * P - n_nodes, D), x.dtype)]),
        "src": edges(src, pad_node), "dst": edges(dst, pad_node), "ew": edges(ew, 0),
        "rbf": np.concatenate([rbf, np.zeros((NG * T * P - n_edges, D), rbf.dtype)]),
        **{f"w_{k}_dram": a for k, a in w.items()},
    }
    nc = bacc.Bacc("TRN2", target_bir_lowering=False, num_devices=1)
    ap = {k: nc.dram_tensor(k, a.shape, mybir.dt.from_np(a.dtype), kind="ExternalInput").ap() for k, a in arrays.items()}
    out = nc.dram_tensor("out", (NB * P, D), F32, kind="ExternalOutput").ap()
    wxh_rows = nc.dram_tensor("wxh_rows", (NBP * P, D), F32).ap()
    x1_rows = nc.dram_tensor("x1_rows", (NB * P, D), F32).ap()
    sorted_rows = nc.dram_tensor("sorted_rows", (NQ * ROWS_Q, W), F32).ap()
    q_block_row = nc.dram_tensor("q_block_row", (1, -(-NQ // P) * P), I32).ap()
    seed_rows = nc.dram_tensor("seed_rows", (S, 16), BF16).ap()
    rel_rows = nc.dram_tensor("rel_rows", (-(-NG * T // P) * P, P), BF16).ap()
    program(nc, n_nodes, n_edges, ap["x"], ap["src"], ap["dst"], ap["ew"], ap["rbf"],
            {k: ap[f"w_{k}_dram"] for k in w}, out, wxh_rows, x1_rows, sorted_rows, q_block_row, seed_rows, rel_rows)
    r = run_bass_kernel_spmd(nc, [arrays], core_ids=[0])
    return r.results[0]["out"][:n_nodes]
```

```python
from contextlib import ExitStack

import concourse.bass as bass
from concourse import mybir

F32 = mybir.dt.float32
BF16 = mybir.dt.bfloat16
I32 = mybir.dt.int32
ALU = mybir.AluOpType
ACT = mybir.ActivationFunctionType
AX = mybir.AxisListType

P = 128
D = 64
T = 8
S = 4
TQ = 4
ROWS_Q = TQ * P
PARTS = 3
SHARE = 2
LOADS = 4
W = D + 1
FAR = float(1 << 20)


def sizes(n_nodes, n_edges):
    blocks = -(-n_nodes // P)
    blocks_padded = -(-blocks // T) * T
    groups = -(-n_edges // (P * T))
    groups = -(-groups // S) * S
    q_groups = (n_edges + blocks * (ROWS_Q - 1)) // ROWS_Q
    q_groups = -(-q_groups // (4 * LOADS)) * (4 * LOADS)
    return blocks, blocks_padded, groups, q_groups


def program(nc, n_nodes, n_edges, x, src, dst, ew, rbf, w, out, wxh_rows, x1_rows, sorted_rows, q_block_row, seed_rows,
            rel_rows):
    NB, NBP, NG, NQ = sizes(n_nodes, n_edges)
    NT = NG * T
    NC = -(-NT // P)
    NGC = -(-NG // P)
    NA = NBP // 8
    HG = 2
    assert NB * 4 <= 2048 and NBP >= NB + 1 and NA * T <= P and NG % (2 * HG) == 0
    QC = -(-NQ // P)
    FR = 32 if 32 * W <= NBP * D else 8
    FILL = sorted_rows.shape[0] // (P * FR)

    ctx = ExitStack()
    with ctx:
        def sb(name, shape, dt=F32):
            return ctx.enter_context(nc.sbuf_tensor(name, shape, dt))

        def pb(name, shape):
            return ctx.enter_context(nc.psum_tensor(name, shape, F32))

        def sem(name):
            return ctx.enter_context(nc.semaphore(name))

        shared = {}

        def shared_sem(name):
            if name not in shared:
                shared[name] = sem(name)
            return shared[name]

        def shared_sem2(name):
            return [shared_sem(f"{name}_{u}") for u in range(2)]

        HELD = 4 * TQ * D // 2
        buffers = max(S * T * (W + D) + S * T * D, (2 * LOADS + 2) * HELD + 2 * TQ * P + 8 * D)
        spaces = [sb(name, [P, max(NBP * D, buffers)]) for name in ("x1_space", "x_space")]
        x1, xs = (a[:, 0:NBP * D].rearrange("p (b d) -> p b d", d=D) for a in spaces)
        agg = sb("agg", [P, NBP, D])

        def carve(layer, *shapes):
            at, found = 0, []
            for n, *dims in shapes:
                size = 1
                for d in dims:
                    size *= d
                names = "abc"[:len(dims)]
                for _ in range(n):
                    a = spaces[layer][:, at:at + size]
                    found.append(a.rearrange(f"p ({' '.join(names)}) -> p {' '.join(names)}",
                                             **dict(zip(names, dims))))
                    at += size
            assert at <= spaces[layer].shape[1]
            return found

        tmp_space = sb("tmp_space", [P, max(NBP * PARTS * D // 2, 4 * LOADS * TQ * W + 2 * LOADS * HELD)])
        tmp = tmp_space[:, 0:NBP * D].rearrange("p (b d) -> p b d", d=D)
        wxh = tmp_space[:, 0:NBP * PARTS * D // 2].bitcast(BF16).rearrange("p (b c d) -> p b c d", c=PARTS, d=D)
        src_i = sb("src_i", [P, NT], I32)
        dst_i = sb("dst_i", [P, NT], I32)
        ew_s = sb("ew_s", [P, NT])
        hi_s = sb("hi_s", [P, NT], BF16)
        lo_s = sb("lo_s", [P, NT], BF16)
        hi_d = sb("hi_d", [P, NT], BF16)
        lo_d = sb("lo_d", [P, NT], BF16)
        far = sb("far", [P, NT], BF16)
        rel = sb("rel", [P, NC * P], BF16)
        rel_bc = [sb(f"rel_bc{u}", [P, T * P], BF16) for u in range(2)]
        window = sb("window", [P, 2 * T * P], BF16)
        window_t = window[:, :].rearrange("p (h n) -> p h n", h=2)
        window_e = window[:, :].rearrange("p (t n) -> p t n", t=T)
        node_iota = sb("node_iota", [P, 2])
        node_iota_i = sb("node_iota_i", [P, 2], I32)
        iota = sb("iota", [P, 2 * P], BF16)
        ident = sb("ident", [P, P])
        ident_b = sb("ident_b", [P, P], BF16)
        ones = sb("ones", [P, P], BF16)
        ones_f = sb("ones_f", [P, P])
        tri = sb("tri", [P, P], BF16)
        before8 = sb("before8", [P, T, T], BF16)
        zeros = sb("zeros", [P, P], BF16)
        row_i = sb("row_i", [P, 2], I32)
        row_f = sb("row_f", [P, 2])
        onehot = [sb(f"onehot{u}", [P, T, NB], BF16) for u in range(2)]
        masked = sb("masked", [P, T, NB])
        run = sb("run", [P, NB])
        base = sb("base", [P, NB])
        cnt = [sb(f"cnt{k}", [P, NB]) for k in range(3)]
        cnt_i = sb("cnt_i", [P, NB], I32)
        same = sb("same", [P, T, T])
        same8 = sb("same8", [P, T])
        rank8 = sb("rank8", [P, T])
        pos = [sb(f"pos{j}", [P, T], I32) for j in range(S)]
        gidx = [sb(f"gidx{j}", [P, T], I32) for j in range(S)]
        in_t = sb("in_t", [P, T * D])
        hid_t = sb("hid_t", [P, T * D])
        f_s = sb("f_s", [P, T, D])
        iota_i = f_s.rearrange("p t d -> p (t d)")[:, 0:2 * P].bitcast(I32)
        rest = sb("rest", [P, T * D])
        q_rows = [tmp_space[:, u * 4 * TQ * W:(u + 1) * 4 * TQ * W].rearrange("p (q t w) -> p q t w", q=4, t=TQ)
                  for u in range(LOADS)]
        q_num_i = sb("q_num_i", [P, QC], I32)
        q_num = sb("q_num", [P, QC])
        q_cmp = sb("q_cmp", [P, QC, NB])
        q_blk = sb("q_blk", [P, QC])
        q_blk_i = sb("q_blk_i", [P, QC], I32)
        q_row = sb("q_row", [1, QC * P], I32)
        stat = [sb(f"stat{k}", [P, NB]) for k in range(2)]
        eps = sb("eps", [P, 1])
        wts = {k: sb(f"w_{k}", list(a.shape)) for k, a in w.items()}
        ends = [sb(f"ends{k}", [P, NGC * P]) for k in range(2)]
        col = sb("col", [P, 1])
        diag = sb("diag", [P, P])
        group_ends = [sb(f"group_ends{k}", [P, NGC * P]) for k in range(2)]
        base_i = sb("base_i", [P, NGC * P], I32)
        local_i = sb("local_i", [P, 1], I32)
        shifted = spaces[0][:, 0:NT].bitcast(I32)
        below = spaces[0][:, NT:2 * NT]
        rel_t = spaces[0][:, 2 * NT:2 * NT + NC * P // 2].bitcast(BF16).rearrange("p (c q) -> p c q", q=P)
        fill_zeros = spaces[0][:, 2 * NT + NC * P // 2:2 * NT + NC * P // 2 + FR * W]

        ps_t = pb("ps_t", [P, T * D])
        ps_h = pb("ps_h", [P, T * D])
        ps_f = pb("ps_f", [P, T * D])
        ps_x = pb("ps_x", [P, T * D])
        ps_rank = pb("ps_rank", [P, 512])
        ps_cnt = pb("ps_cnt", [P, 512])
        ps_agg = [pb(f"ps_agg{u}", [P, 512]) for u in range(2)]
        ps_win = [ps_agg, [ps_t, ps_h]]

        def count_of(i, j, back=0):
            return i * S + (S + 1 + j - back)

        def seed(e, *sems, n=S):
            for s in sems:
                e.sem_inc(s, n)

        def stepper(e, s, n=0):
            n = [n]

            def step(ins):
                ins.then_inc(s, 1)
                n[0] += 1
                e.wait_ge(s, n[0])
            return step

        def by_locality(e, local, other):
            flag = e.value_load(local_i[0:1, 0:1], min_val=0, max_val=1)
            with e.If(flag > 0):
                local()
            with e.Else():
                other()

        def counting(layer, hi):
            c_oh, c_mm = shared_sem2("c_oh"), shared_sem2("c_mm")
            c_zero, c_tot, c_d = (shared_sem(f"c_{k}") for k in ("zero", "tot", "d"))
            c_dma, c_dma2 = (sem(f"c{layer}_{k}") for k in ("dma", "dma2"))

            eighth_i = spaces[layer][:, 0:NT].bitcast(I32)
            eighth, place = (spaces[layer][:, NT + k * (NT // 2):NT + (k + 1) * (NT // 2)].bitcast(BF16)
                             for k in range(2))
            eighth_of = [window[:, u * HG * NA * T:(u + 1) * HG * NA * T].rearrange("p (g a t) -> p g a t", g=HG, t=T)
                         for u in range(2)]
            place_of = [rel_bc[u][:, 0:HG * 8 * T].rearrange("p (g b t) -> p g b t", g=HG, t=T) for u in range(2)]
            pair, at_block, block_of, spread = (hid_t[0:NA * T, a:b] for a, b in (
                (0, 8 * T), (8 * T, 8 * T + 8), (8 * T + 8, 8 * T + 8 + NA), (9 * T + 8 + NA, 9 * T + 8 + NA + NBP)))

            def vector(e):
                step = stepper(e, c_d)
                step(e.tensor_copy(eighth_i, hi[:, :]))
                step(e.tensor_scalar(eighth_i, eighth_i, 3, None, ALU.logical_shift_right))
                step(e.tensor_copy(eighth, eighth_i))
                step(e.tensor_copy(eighth_i, hi[:, :]))
                step(e.tensor_scalar(eighth_i, eighth_i, 7, None, ALU.bitwise_and))
                step(e.tensor_copy(place, eighth_i))
                with e.Fori(0, NG // (2 * HG)) as i:
                    for u in range(2):
                        e.wait_ge(c_mm[u], i + 1)
                        for n, of, to in ((NA, eighth, eighth_of), (8, place, place_of)):
                            tiles_ = of[:, bass.ds(i * (2 * HG * T) + u * HG * T, HG * T)]
                            last = e.tensor_tensor(
                                to[u][:, :, :, :],
                                tiles_.rearrange("p (g t) -> p g t", t=T).unsqueeze(2).broadcast_to([P, HG, n, T]),
                                iota[:, 0:n].unsqueeze(1).unsqueeze(3).broadcast_to([P, HG, n, T]), ALU.is_equal)
                        last.then_inc(c_oh[u], 1)
                e.wait_ge(c_tot, 1)
                for k, op, by in ((0, ALU.bitwise_and, T - 1), (1, ALU.logical_shift_right, T.bit_length() - 1)):
                    step(e.tensor_scalar(row_i[:, k:k + 1], node_iota_i[:, 0:1], by, None, op))
                    step(e.tensor_copy(row_f[:, k:k + 1], row_i[:, k:k + 1]))
                M = NA * T
                step(e.tensor_scalar(at_block, iota[0:M, 0:T], row_f[0:M, 0:1], None, ALU.is_equal))
                step(e.tensor_tensor(pair.rearrange("p (b t) -> p b t", t=T),
                                     ps_cnt[0:M, 0:8 * T].rearrange("p (b t) -> p b t", t=T),
                                     at_block[:, None, :].broadcast_to([M, 8, T]), ALU.mult))
                step(e.tensor_reduce(at_block, pair.rearrange("p (b t) -> p b t", t=T), AX.X, ALU.add))
                step(e.tensor_scalar(block_of, iota[0:M, 0:NA], row_f[0:M, 1:2], None, ALU.is_equal))
                step(e.tensor_tensor(spread.rearrange("p (a b) -> p a b", b=8),
                                     block_of.unsqueeze(2).broadcast_to([M, NA, 8]),
                                     at_block[:, None, :].broadcast_to([M, NA, 8]), ALU.mult))
                e.wait_ge(c_tot, 2)
                step(e.tensor_copy(cnt[0][:, :], ps_rank[:, 0:NB]))
                step(e.tensor_scalar(cnt[0][:, :], cnt[0][:, :], float(ROWS_Q - 1), None, ALU.add))
                step(e.tensor_copy(cnt_i[:, :], cnt[0][:, :]))
                step(e.tensor_scalar(cnt_i[:, :], cnt_i[:, :], ROWS_Q.bit_length() - 1, None,
                                     ALU.logical_shift_right))
                step(e.tensor_copy(cnt[0][:, :], cnt_i[:, :]))
                a, b = cnt[1], cnt[2]
                step(e.tensor_copy(a[:, :], cnt[0][:, :]))
                k = 1
                while k < NB:
                    step(e.tensor_copy(b[:, 0:k], a[:, 0:k]))
                    step(e.tensor_tensor(b[:, k:NB], a[:, k:NB], a[:, 0:NB - k], ALU.add))
                    a, b = b, a
                    k *= 2
                step(e.tensor_tensor(
                    q_cmp[:, :, :], a[:, None, :].broadcast_to([P, QC, NB]),
                    q_num[:, :].unsqueeze(2).broadcast_to([P, QC, NB]), ALU.is_le))
                step(e.tensor_reduce(q_blk[:, :], q_cmp[:, :, :], AX.X, ALU.add))
                step(e.tensor_copy(q_blk_i[:, :], q_blk[:, :]))
                step(e.tensor_tensor(b[:, :], a[:, :], cnt[0][:, :], ALU.subtract))
                step(e.tensor_scalar(run[:, :], b[:, :], float(ROWS_Q), None, ALU.mult))

            n_spread = 6 + 4 + 5
            n_steps = n_spread + 6 + 2 * (NB - 1).bit_length() + 5

            def tensor(e):
                seed(e, *c_mm, n=1)
                counts = ps_cnt[0:NA * T, 0:8 * T]
                e.matmul(counts, zeros[:, 0:NA * T], zeros[:, 0:8 * T], start=True, stop=False).then_inc(c_zero, 1)
                with e.Fori(0, NG // (2 * HG)) as i:
                    for u in range(2):
                        e.wait_ge(c_oh[u], i + 1)
                        for g in range(HG):
                            last = e.matmul(counts, eighth_of[u][:, g, :, :].rearrange("p a t -> p (a t)"),
                                            place_of[u][:, g, :, :].rearrange("p b t -> p (b t)"),
                                            start=False, stop=False)
                        last.then_inc(c_mm[u], 1)
                e.matmul(counts, zeros[:, 0:NA * T], zeros[:, 0:8 * T], start=False, stop=True).then_inc(c_tot, 1)
                e.wait_ge(c_d, n_spread)
                e.matmul(ps_rank[:, 0:NBP], ones_f[0:NA * T, :], spread, start=True, stop=True).then_inc(c_tot, 1)

            def scalar(e):
                e.wait_ge(c_d, n_steps)
                with nc.allow_non_contiguous_dma(reason="a few hundred words"):
                    e.dma_start(q_block_row[0, :].rearrange("(c p) -> p c", p=P), q_blk_i[:, :]).then_inc(c_dma, 16)
                e.wait_ge(c_dma, 16)
                e.dma_start(q_row[:, :], q_block_row).then_inc(c_dma2, 16)
                e.wait_ge(c_dma2, 16)

            return vector, tensor, scalar

        s_const, s_in, s_x, s_zero, s_fill, s_d, s_pool = (
            sem(f"s_{k}") for k in ("const", "in", "x", "zero", "fill", "d", "pool"))
        w_t, w_ev, w_f, w_b, w_add, w_hi, w_r1, w_mid, w_lo = (
            sem(f"wxh_{k}") for k in ("t", "ev", "f", "b", "add", "hi", "r1", "mid", "lo"))
        w_out = sem("wxh_out")
        wxh_f = agg[:, :, :]
        g_t, g_bc, r_t, r_ev, r_out = (sem(k) for k in ("ends_t", "ends_bc", "rel_t_", "rel_ev", "rel_out"))
        fill = sorted_rows.rearrange("(c p r) w -> c p (r w)", p=P, r=FR)
        GN = NBP // T
        KEYS = 3 + 9
        ENDS = KEYS + 4
        REL = ENDS + 2 * NGC * 3 + 7

        def set_up(count):
            c_vector, c_tensor, c_scalar = count
            with nc.Block() as block:
                @block.gpsimd
                def _(e):
                    e.iota(iota_i, pattern=[[1, 2 * P]], base=0, channel_multiplier=0).then_inc(s_pool, 1)
                    e.iota(node_iota_i[:, :], pattern=[[P, 2]], base=0, channel_multiplier=1).then_inc(s_pool, 1)
                    e.iota(q_num_i[:, :], pattern=[[P, QC]], base=0, channel_multiplier=1).then_inc(s_pool, 1)
                    for t, v in ((ident, 0.0), (ident_b, 0.0), (ones, 1.0), (ones_f, 1.0), (zeros, 0.0),
                                 (eps, 1e-5), (local_i, 0), (rel, 0.0), (ends[0], 0.0), (ends[1], 0.0)):
                        e.memset(t[:, :], v).then_inc(s_pool, 1)
                    e.memset(before8[:, :, :], 1.0).then_inc(s_pool, 1)
                    e.wait_ge(s_pool, 14)
                    for t in (ident, ident_b):
                        e.affine_select(out=t[:, :], in_=t[:, :], compare_op=ALU.not_equal, fill=1.0,
                                        base=0, pattern=[[-1, P]], channel_multiplier=1).then_inc(s_const, 1)
                    e.affine_select(out=tri[:, :], in_=ones[:, :], compare_op=ALU.is_gt, fill=0.0,
                                    base=0, pattern=[[1, P]], channel_multiplier=-1).then_inc(s_const, 1)
                    e.affine_select(out=before8[:, :, :], in_=before8[:, :, :], compare_op=ALU.is_gt, fill=0.0,
                                    base=0, pattern=[[1, T], [-1, T]], channel_multiplier=0).then_inc(s_const, 1)
                    e.wait_ge(w_add, GN)

                    @unless_local
                    def store(e):
                        e.dma_start(wxh_rows.rearrange("(b p) d -> p b d", p=P), wxh_f).then_inc(w_out, 16)
                        e.wait_ge(w_out, 16)
                    store(e)

                @block.sync
                def _(e):
                    for t, a in ((src_i, src), (dst_i, dst), (ew_s, ew)):
                        e.dma_start(t[:, :], a).then_inc(s_in, 16)
                    e.dma_start(xs[:, :, :], x.rearrange("(b p) d -> p b d", p=P)).then_inc(s_x, 16)
                    e.wait_ge(s_zero, 1)
                    with e.Fori(0, FILL) as c:
                        e.dma_start(fill[bass.ds(c, 1), :, :].rearrange("c p n -> (c p) n"), fill_zeros
                                    ).then_inc(s_fill, 16)
                    e.wait_ge(s_fill, 16 * FILL)

                @block.scalar
                def _(e):
                    for k, a in w.items():
                        e.dma_start(wts[k][:, :], a).then_inc(w_b, 16)
                    for c in range(NC):
                        e.wait_ge(r_t, c + 1)
                        e.copy(rel_t[:, c, :], ps_x[:, 0:P // 2].bitcast(BF16)).then_inc(r_ev, 1)
                    e.wait_ge(r_ev, NC)
                    e.dma_start(rel_rows.rearrange("(c t) p -> t c p", t=P), rel_t).then_inc(r_out, 16)
                    for g in range(GN):
                        e.wait_ge(w_t, g + 1)
                        e.wait_ge(w_f, g)
                        e.copy(in_t[:, :], ps_t[:, :]).then_inc(w_ev, 1)
                        for h in ((g - 1,) if g else ()) + ((g,) if g == GN - 1 else ()):
                            e.wait_ge(w_add, h + 1)
                            e.copy(wxh[:, h * T:(h + 1) * T, 0, :], wxh_f[:, h * T:(h + 1) * T, :]).then_inc(w_hi, 1)
                            e.wait_ge(w_r1, h + 1)
                            e.copy(wxh[:, h * T:(h + 1) * T, 1, :], f_s[:, :, :]).then_inc(w_mid, 1)
                    c_scalar(e)
                    e.wait_ge(r_out, 16)

                @block.tensor
                def _(e):
                    e.wait_ge(s_const, 4)
                    e.wait_ge(s_x, 16)
                    e.wait_ge(w_b, 16 * len(w))
                    at = ENDS
                    for k in range(2):
                        for c in range(NGC):
                            e.wait_ge(s_d, at)
                            e.transpose(ps_h[:, 0:P], ends[k][:, c * P:(c + 1) * P], ident[:, :]).then_inc(g_t, 1)
                            e.wait_ge(s_d, at + 2)
                            e.matmul(ps_h[:, P:2 * P], ones_f[:, :], diag[:, :],
                                     start=True, stop=True).then_inc(g_bc, 1)
                            at += 3
                    e.wait_ge(s_d, REL)
                    for c in range(NC):
                        e.wait_ge(r_ev, c)
                        e.transpose(ps_x[:, 0:P // 2].bitcast(BF16), rel[:, c * P:(c + 1) * P],
                                    ident_b[:, :]).then_inc(r_t, 1)
                    for g in range(GN):
                        e.wait_ge(w_ev, g)
                        for k in range(T // 2):
                            pair = xs[:, g * T + 2 * k:g * T + 2 * k + 2, :].rearrange("p b d -> p (b d)")
                            last = e.transpose(ps_t[:, k * P:(k + 1) * P], pair, ident[:, :])
                        last.then_inc(w_t, 1)
                        e.wait_ge(w_ev, g + 1)
                        e.wait_ge(w_add, g)
                        for k in range(T // 2):
                            last = e.matmul(ps_f[:, k * P:(k + 1) * P], in_t[:, k * P:(k + 1) * P],
                                            wts["wl"][:, :], start=True, stop=True)
                        last.then_inc(w_f, 1)
                    c_tensor(e)

                @block.vector
                def _(e):
                    e.memset(fill_zeros, 0.0).then_inc(s_zero, 1)
                    step = stepper(e, s_d)
                    e.wait_ge(s_pool, 14)
                    step(e.tensor_copy(iota[:, :], iota_i))
                    step(e.tensor_copy(q_num[:, :], q_num_i[:, :]))
                    step(e.tensor_copy(node_iota[:, :], node_iota_i[:, :]))
                    e.wait_ge(s_in, 48)
                    for a, hi, lo in ((src_i, hi_s, lo_s), (dst_i, hi_d, lo_d)):
                        step(e.tensor_scalar(shifted, a[:, :], 7, None, ALU.logical_shift_right))
                        step(e.tensor_copy(hi[:, :], shifted))
                        step(e.tensor_scalar(shifted, a[:, :], P - 1, None, ALU.bitwise_and))
                        step(e.tensor_copy(lo[:, :], shifted))
                    step(e.tensor_scalar(far[:, :], hi_s[:, :], float(NB), FAR, ALU.is_ge, ALU.mult))
                    grouped = lambda a: a.rearrange("p (g t) -> p g t", t=T)
                    step(e.tensor_reduce(ends[0][:, 0:NG], grouped(hi_d[:, :]), AX.X, ALU.min))
                    step(e.tensor_scalar(below, hi_d[:, :], float(NB), None, ALU.is_lt))
                    step(e.tensor_tensor(below, below, hi_d[:, :], ALU.mult))
                    step(e.tensor_reduce(ends[1][:, 0:NG], grouped(below), AX.X, ALU.max))
                    n = 0
                    for k, op in enumerate((ALU.min, ALU.max)):
                        for c in range(NGC):
                            n += 1
                            e.wait_ge(g_t, n)
                            step(e.tensor_reduce(col[:, :], ps_h[:, 0:P], AX.X, op))
                            step(e.tensor_scalar(diag[:, :], ident[:, :], col[:, 0:1], None, ALU.mult))
                            e.wait_ge(g_bc, n)
                            step(e.tensor_copy(group_ends[k][:, c * P:(c + 1) * P], ps_h[:, P:2 * P]))
                    first, last = (t[:, 0:NG] for t in group_ends)
                    spread = ends[0][:, 0:NG]
                    step(e.tensor_tensor(spread, last, first, ALU.subtract))
                    step(e.tensor_reduce(col[:, :], spread, AX.X, ALU.max))
                    step(e.tensor_scalar(local_i[:, :], col[:, :], 1.5, None, ALU.is_lt))
                    step(e.tensor_scalar(first, first, float(NB - 1), None, ALU.min))
                    step(e.tensor_copy(base_i[:, 0:NG], first))
                    step(e.tensor_tensor(grouped(below), grouped(hi_d[:, :]),
                                         first.unsqueeze(2).broadcast_to([P, NG, T]), ALU.subtract))
                    step(e.scalar_tensor_tensor(out=rel[:, 0:NT], in0=below, scalar=float(P), in1=lo_d[:, :],
                                                op0=ALU.mult, op1=ALU.add))
                    for g in range(GN):
                        blocks = slice(g * T, (g + 1) * T)
                        e.wait_ge(w_f, g + 1)
                        e.tensor_tensor(wxh_f[:, blocks, :], ps_f[:, :].rearrange("p (t d) -> p t d", d=D),
                                        wts["bl"][:, None, :].broadcast_to([P, T, D]), ALU.add).then_inc(w_add, 1)
                        e.wait_ge(w_lo, g)
                        e.wait_ge(w_hi, g + 1)
                        e.tensor_tensor(f_s[:, :, :], wxh_f[:, blocks, :], wxh[:, blocks, 0, :],
                                        ALU.subtract).then_inc(w_r1, 1)
                        e.wait_ge(w_mid, g + 1)
                        e.tensor_tensor(wxh[:, blocks, 2, :], f_s[:, :, :], wxh[:, blocks, 1, :],
                                        ALU.subtract).then_inc(w_lo, 1)
                    c_vector(e)

        def count_again(layer, hi):
            vector, tensor, scalar = counting(layer, hi)
            with nc.Block() as block:
                block.vector(unless_local(vector))
                block.tensor(unless_local(tensor))
                block.scalar(unless_local(scalar))

        def unless_local(body):
            def run_(e):
                flag = e.value_load(local_i[0:1, 0:1], min_val=0, max_val=1)
                with e.If(flag < 1):
                    body(e)
            return run_

        def messages(layer, hi, lo, idx, table):
            rows_, gathered_, rbf_ = (S, T, W), (S, T, D), (S, T * D)
            found = carve(layer, rows_, gathered_, rbf_)
            rows, gathered, rbf_s = found[0:S], found[S:2 * S], found[2 * S:3 * S]
            xg, sc, ld, rl = ([sem(f"m{layer}_{k}_{j}") for j in range(S)] if k in ("xg", "sc") or layer == 0 else None
                              for k in ("xg", "sc", "ld", "rl"))
            gi, m, lo_w, oh, rk, bs, rn, ww, pr, pr2, c1, c2, c3, po, tr, ev, h1, si, f2, f1, wi, xw = (
                shared_sem(f"m_{k}") for k in (
                    "gi", "m", "lo", "oh", "rk", "bs", "rn", "ww", "pr", "pr2", "c1", "c2", "c3", "po",
                    "tr", "ev", "h1", "si", "f2", "f1", "wi", "xw"))
            passes = NG // S
            tiles = lambda i, j: bass.ds(i * (S * T) + j * T, T)

            def sync(e, local):
                r = rbf.rearrange("(g p t) k -> g p (t k)", p=P, t=T)
                q = rel_rows[0:NT, :].rearrange("(g t) p -> g (t p)", t=T)
                with e.Fori(0, passes) as i:
                    for j in range(S):
                        e.wait_ge(tr, count_of(i, j, S))
                        e.dma_start(rbf_s[j], r[bass.ds(i * S + j, 1), :, :].rearrange("g p n -> (g p) n")
                                    ).then_inc(ld[j], 16)
                        if local:
                            e.wait_ge(wi, count_of(i, j, 2))
                            e.dma_start(rel_bc[j % 2][:, :], q[bass.ds(i * S + j, 1), :].broadcast_to([P, T * P])
                                        ).then_inc(rl[j], 16)

            def scalar(e):
                with e.Fori(0, passes) as i:
                    for j in range(S):
                        if layer == 0:
                            e.wait_ge(h1, count_of(i, j, 1))
                            e.wait_ge(tr, count_of(i, j))
                            e.copy(in_t[:, :], ps_t[:, :]).then_inc(ev, 1)
                        e.wait_ge(sc[j], i * (16 * T) + 16 * T)
                        e.copy(rows[j][:, :, D], lo[:, tiles(i, j)]).then_inc(lo_w, 1)
                        if layer == 0:
                            e.wait_ge(f2, count_of(i, j, 1))
                            e.wait_ge(h1, count_of(i, j))
                            e.activation(hid_t[:, :], ps_h[:, :], ACT.Silu, bias=wts["bf1"][:, 0:1]).then_inc(si, 1)
                if layer == 0:
                    e.copy(agg[:, :, :], xs[:, :, :])

            def tensor(e, local):
                with e.Fori(0, passes) as i:
                    for j in range(S):
                        if layer == 0:
                            e.wait_ge(ld[j], i * 16 + 16)
                            e.wait_ge(ev, count_of(i, j, 1))
                            for t in range(T // 2):
                                last = e.transpose(ps_t[:, t * P:(t + 1) * P],
                                                   rbf_s[j][:, t * P:(t + 1) * P], ident[:, :])
                            last.then_inc(tr, 1)
                        e.wait_ge(rn, count_of(i, j, 1))
                        e.wait_ge(oh, count_of(i, j))
                        for t in range(T):
                            e.matmul(ps_rank[:, 0:NB], tri[:, :], onehot[j % 2][:, t, :],
                                     start=(t == 0), stop=(t == T - 1))
                        for t in range(T):
                            last = e.matmul(ps_cnt[:, 0:NB], ones[:, :], onehot[j % 2][:, t, :],
                                            start=(t == 0), stop=(t == T - 1))
                        last.then_inc(rk, 1)
                        if layer:
                            continue
                        e.wait_ge(si, count_of(i, j, 1))
                        e.wait_ge(ev, count_of(i, j))
                        e.matmul(ps_h[:, :], wts["wf1"][:, :], in_t[:, :], start=True, stop=True).then_inc(h1, 1)
                        if local:
                            b = e.value_load(base_i[0:1, bass.ds(i * S + j, 1)], min_val=0, max_val=NB - 1)
                            e.wait_ge(m, count_of(i, j, 1))
                            e.wait_ge(wi, count_of(i, j))
                            for t in range(T):
                                for h in range(2):
                                    for c in range(PARTS):
                                        last = e.matmul(
                                            ps_x[:, t * D:(t + 1) * D], window_t[:, h, t * P:(t + 1) * P],
                                            wxh[:, bass.ds(b + h, 1), c, :].rearrange("p b d -> p (b d)"),
                                            start=(h == 0 and c == 0), stop=(h == 1 and c == PARTS - 1))
                            last.then_inc(xw, 1)
                        e.wait_ge(f1, count_of(i, j, 1))
                        e.wait_ge(si, count_of(i, j))
                        for t in range(T // 2):
                            last = e.matmul(ps_f[:, t * P:(t + 1) * P], hid_t[:, t * P:(t + 1) * P],
                                            wts["wf2"][:, :], start=True, stop=True)
                        last.then_inc(f2, 1)

            def vector(e, local):
                with e.Fori(0, passes) as i:
                    for j in range(S):
                        at = tiles(i, j)
                        if not local:
                            e.wait_ge(m, count_of(i, j, S))
                            e.tensor_copy(gidx[j][:, :], idx[:, at]).then_inc(gi, 1)
                        e.wait_ge(rk, count_of(i, j, 2))
                        e.wait_ge(ww, count_of(i, j, 2))
                        e.tensor_tensor(onehot[j % 2][:, :, :], hi[:, at].unsqueeze(2).broadcast_to([P, T, NB]),
                                        iota[:, None, 0:NB].broadcast_to([P, T, NB]), ALU.is_equal).then_inc(oh, 1)
                        if local:
                            e.wait_ge(rl[j], i * 16 + 16)
                            e.wait_ge(xw, count_of(i, j, 1))
                            for h in range(2):
                                last = e.tensor_scalar(window_t[:, h, :], rel_bc[j % 2][:, :],
                                                       node_iota[:, h:h + 1], None, ALU.is_equal)
                            last.then_inc(wi, 1)
                        e.wait_ge(c3, count_of(i, j, 1))
                        e.tensor_tensor(same[:, :, :], hi[:, at].unsqueeze(2).broadcast_to([P, T, T]),
                                        hi[:, at].unsqueeze(1).broadcast_to([P, T, T]), ALU.is_equal).then_inc(c1, 1)
                        e.wait_ge(c1, count_of(i, j))
                        e.tensor_tensor(same[:, :, :], same[:, :, :], before8[:, :, :], ALU.mult).then_inc(c2, 1)
                        e.wait_ge(po, count_of(i, j, 1))
                        e.wait_ge(c2, count_of(i, j))
                        e.tensor_reduce(same8[:, :], same[:, :, :], AX.X, ALU.add).then_inc(c3, 1)
                        e.wait_ge(ww, count_of(i, j, 1))
                        e.wait_ge(rn, count_of(i, j, 1))
                        e.wait_ge(rk, count_of(i, j))
                        e.tensor_tensor(base[:, :], run[:, :], ps_rank[:, 0:NB], ALU.add).then_inc(bs, 1)
                        e.wait_ge(bs, count_of(i, j))
                        e.tensor_tensor(run[:, :], run[:, :], ps_cnt[:, 0:NB], ALU.add).then_inc(rn, 1)
                        e.wait_ge(pr, count_of(i, j, 1))
                        e.tensor_tensor(masked[:, :, :], onehot[j % 2][:, :, :],
                                        base[:, None, :].broadcast_to([P, T, NB]), ALU.mult).then_inc(ww, 1)
                        e.wait_ge(c3, count_of(i, j))
                        e.wait_ge(ww, count_of(i, j))
                        e.tensor_reduce(rank8[:, :], masked[:, :, :], AX.X, ALU.add).then_inc(pr, 1)
                        e.wait_ge(pr, count_of(i, j))
                        e.tensor_tensor(rank8[:, :], rank8[:, :], same8[:, :], ALU.add).then_inc(pr2, 1)
                        e.wait_ge(sc[j], i * (16 * T) + 16 * T)
                        e.wait_ge(pr2, count_of(i, j))
                        e.tensor_tensor(pos[j][:, :], rank8[:, :], far[:, at], ALU.add).then_inc(po, 1)
                        if layer == 0:
                            e.wait_ge(m, count_of(i, j, 1))
                            e.wait_ge(f2, count_of(i, j))
                            e.tensor_tensor(f_s[:, :, :], ps_f[:, :].rearrange("p (t d) -> p t d", d=D),
                                            wts["bf2"][:, None, :].broadcast_to([P, T, D]), ALU.add).then_inc(f1, 1)
                            e.wait_ge(f1, count_of(i, j))
                        if local:
                            e.wait_ge(xw, count_of(i, j))
                            rows_in = ps_x[:, :].rearrange("p (t d) -> p t d", d=D)
                        else:
                            e.wait_ge(xg[j], i * (16 * T) + 16 * T)
                            rows_in = gathered[j]
                        other = f_s[:, :, :] if layer == 0 else ew_s[:, at].unsqueeze(2).broadcast_to([P, T, D])
                        e.tensor_tensor(rows[j][:, :, 0:D], rows_in, other, ALU.mult).then_inc(m, 1)

            def gpsimd(e, local):
                def gather(j, i):
                    if local:
                        return
                    e.wait_ge(m, count_of(i, j, S))
                    e.wait_ge(gi, count_of(i, j))
                    e.sem_inc(s_go, 1)
                    for t in range(T):
                        e.indirect_dma_start(
                            out=gathered[j][:, t, :], out_offset=None, in_=table,
                            in_offset=bass.IndirectOffsetOnAxis(ap=gidx[j][:, t:t + 1], axis=0),
                            bounds_check=n_nodes - 1, oob_is_err=False).then_inc(xg[j], 16)

                def scatter(j, i):
                    e.wait_ge(m, count_of(i, j))
                    e.wait_ge(lo_w, count_of(i, j))
                    e.wait_ge(po, count_of(i, j))
                    e.sem_inc(s_go, 1)
                    for t in range(T):
                        e.indirect_dma_start(
                            out=sorted_rows, out_offset=bass.IndirectOffsetOnAxis(ap=pos[j][:, t:t + 1], axis=0),
                            in_=rows[j][:, t, :], in_offset=None,
                            bounds_check=NQ * ROWS_Q - 1, oob_is_err=False).then_inc(sc[j], 16)

                gather(0, 0)
                with e.Fori(0, passes - 1) as i:
                    for j in range(S):
                        gather((j + 1) % S, i + (j + 1) // S)
                        scatter(j, i)
                i = passes - 1
                for j in range(S):
                    if j + 1 < S:
                        gather(j + 1, i)
                    scatter(j, i)

            with nc.Block() as block:
                def part(seeds, body, takes_local=True):
                    def run_(e):
                        seed(e, *seeds)
                        if not takes_local:
                            return body(e) if layer == 0 else unless_local(body)(e)
                        if layer:
                            return unless_local(lambda e: body(e, False))(e)
                        by_locality(e, lambda: body(e, True), lambda: body(e, False))
                    return run_

                zero = layer == 0
                if zero:
                    block.sync(part((), sync))
                block.scalar(part((ev, si, lo_w), scalar, takes_local=False))
                block.tensor(part((rk, tr, h1, f2, xw), tensor))
                block.vector(part((gi, oh, wi, c1, c2, c3, bs, rn, ww, pr, pr2, po, f1, m), vector))

                @block.gpsimd
                def _(e):
                    for j in range(S):
                        e.memset(gathered[j], 0.0).then_inc(s_pad, 1)
                    e.wait_ge(s_pad, S * (layer + 1))
                    for j in range(S):
                        e.dma_start(seed_rows[j:j + 1, :], zeros[0:1, 0:16]).then_inc(sc[j], 16 * T)
                    for j in range(S):
                        e.wait_ge(sc[j], 16 * T)
                    part((), gpsimd)(e)

                    def all_scattered(e):
                        for j in range(S):
                            e.wait_ge(sc[j], 16 * T * (passes + 1))

                    def all_gathered(e):
                        for j in range(S):
                            e.wait_ge(xg[j], 16 * T * passes)
                    (all_scattered if zero else unless_local(all_scattered))(e)
                    unless_local(all_gathered)(e)

        def window_sums():
            found = carve(1, (S, T, D), (2, T, D), (2, T, D // 2), (2, T, D // 2), (2, T, D // 2))
            gathered, msg, parts = found[0:S], found[S:S + 2], found[S + 2:]
            parts = [[parts[2 * c + k].bitcast(BF16) for c in range(PARTS)] for k in range(2)]
            xg = [sem(f"l1_xg_{j}") for j in range(S)]
            gi, m, wi, mm, ac, p1, r1, p2, p3 = (
                sem(f"l1_{k}") for k in ("gi", "m", "wi", "mm", "ac", "p1", "r1", "p2", "p3"))
            passes = NG // S
            tiles = lambda i, j: bass.ds(i * (S * T) + j * T, T)

            def vector(e):
                def indices(i, j):
                    e.wait_ge(m, count_of(i, j, S))
                    e.tensor_copy(gidx[j][:, :], src_i[:, tiles(i, j)]).then_inc(gi, 1)

                def make_parts(i, j):
                    at = tiles(i, j)
                    e.wait_ge(xg[j], i * (16 * T) + 16 * T)
                    e.wait_ge(p1, count_of(i, j, 2))
                    e.wait_ge(r1, count_of(i, j, 2))
                    e.tensor_tensor(msg[j % 2], gathered[j],
                                    ew_s[:, at].unsqueeze(2).broadcast_to([P, T, D]), ALU.mult).then_inc(m, 1)
                    e.wait_ge(p1, count_of(i, j))
                    e.wait_ge(p3, count_of(i, j, 1))
                    e.tensor_tensor(rest[:, :].rearrange("p (t d) -> p t d", d=D), msg[j % 2], parts[j % 2][0],
                                    ALU.subtract).then_inc(r1, 1)
                    e.wait_ge(p2, count_of(i, j))
                    e.tensor_tensor(parts[j % 2][2], rest[:, :].rearrange("p (t d) -> p t d", d=D), parts[j % 2][1],
                                    ALU.subtract).then_inc(p3, 1)

                def make_window(i, j):
                    e.wait_ge(mm, count_of(i, j, 1))
                    e.tensor_tensor(window_e, rel[:, tiles(i, j)].unsqueeze(2).broadcast_to([P, T, 2 * P]),
                                    iota[:, None, :].broadcast_to([P, T, 2 * P]), ALU.is_equal).then_inc(wi, 1)

                def add(i, j):
                    b = e.value_load(base_i[0:1, bass.ds(i * S + j, 1)], min_val=0, max_val=NB - 1)
                    e.wait_ge(mm, count_of(i, j))
                    e.wait_ge(ac, count_of(i, j, 1))
                    for h in range(2):
                        to = agg[:, bass.ds(b + h, 1), :].rearrange("p b d -> p (b d)")
                        last = e.tensor_tensor(to, to, ps_win[j % 2][h][:, 0:D], ALU.add)
                    last.then_inc(ac, 1)

                def sums(i, ahead):
                    for j in range(S):
                        make_parts(i, j)
                        if ahead:
                            indices(i + 1, j)
                        if j:
                            add(i, j - 1)
                        make_window(i, j)
                    add(i, S - 1)

                for j in range(S):
                    indices(0, j)
                with e.Fori(0, passes - 1) as i:
                    sums(i, True)
                sums(passes - 1, False)

            def tensor(e):
                with e.Fori(0, passes) as i:
                    for j in range(S):
                        e.wait_ge(ac, count_of(i, j, 2))
                        e.wait_ge(wi, count_of(i, j))
                        e.wait_ge(p3, count_of(i, j))
                        for h in range(2):
                            for t in range(T):
                                for c in range(PARTS):
                                    last = e.matmul(ps_win[j % 2][h][:, 0:D], window_e[:, t, h * P:(h + 1) * P],
                                                    parts[j % 2][c][:, t, :], start=(t == 0 and c == 0),
                                                    stop=(t == T - 1 and c == PARTS - 1))
                        last.then_inc(mm, 1)

            def scalar(e):
                with e.Fori(0, passes) as i:
                    for j in range(S):
                        e.wait_ge(mm, count_of(i, j, 2))
                        e.wait_ge(m, count_of(i, j))
                        e.copy(parts[j % 2][0], msg[j % 2]).then_inc(p1, 1)
                        e.wait_ge(r1, count_of(i, j))
                        e.copy(parts[j % 2][1], rest[:, :].rearrange("p (t d) -> p t d", d=D)).then_inc(p2, 1)

            def gpsimd(e):
                for j in range(S):
                    e.memset(gathered[j], 0.0).then_inc(s_pad, 1)
                e.wait_ge(s_pad, 2 * S)
                with e.Fori(0, passes) as i:
                    for j in range(S):
                        e.wait_ge(m, count_of(i, j, S))
                        e.wait_ge(gi, count_of(i, j))
                        e.sem_inc(s_go, 1)
                        for t in range(T):
                            e.indirect_dma_start(
                                out=gathered[j][:, t, :], out_offset=None, in_=x1_rows,
                                in_offset=bass.IndirectOffsetOnAxis(ap=gidx[j][:, t:t + 1], axis=0),
                                bounds_check=n_nodes - 1, oob_is_err=False).then_inc(xg[j], 16)
                for j in range(S):
                    e.wait_ge(xg[j], 16 * T * passes)

            with nc.Block() as block:
                def part(seeds, body):
                    def run_(e):
                        seed(e, *seeds)
                        flag = e.value_load(local_i[0:1, 0:1], min_val=0, max_val=1)
                        with e.If(flag > 0):
                            body(e)
                    return run_
                block.vector(part((gi, m, wi, ac, r1, p3), vector))
                block.scalar(part((p1, p2), scalar))
                block.tensor(part((mm,), tensor))
                block.gpsimd(part((), gpsimd))

        def reduce_rows(layer):
            found = carve(layer, (2, HELD), (LOADS, 2 * HELD), (2, TQ * P), (2, 4, D))
            rows_of = lambda a: a.rearrange("p (n d) -> p n d", d=D)
            at = 4 * LOADS * TQ * W
            early = [tmp_space[:, at + n * HELD:at + (n + 1) * HELD] for n in range(2 * LOADS)]
            parts = [[rows_of(a.bitcast(BF16)) for a in (early[u], early[LOADS + u], found[u % 2])]
                     for u in range(LOADS)]
            left = [rows_of(a) for a in found[2:2 + LOADS]]
            q_onehot = [a.bitcast(BF16).rearrange("p (t n) -> p t n", t=2 * TQ) for a in found[2 + LOADS:4 + LOADS]]
            sums = found[4 + LOADS:]
            slot_sums = lambda u: ps_agg[u % 2][:, 0:4 * D].rearrange("p (q d) -> p q d", d=D)
            data = [a.rearrange("p q t w -> p (q t) w")[:, :, 0:D] for a in q_rows]
            ld = [sem(f"r{layer}_ld{u}") for u in range(LOADS)]
            oh, mm, ev, ac, p1, p2, p3, r1, r1_v = (
                shared_sem(f"r_{k}") for k in ("oh", "mm", "ev", "ac", "p1", "p2", "p3", "r1", "r1_v"))
            pool_tiles, vector_tiles = slice(0, 4 * TQ - SHARE), slice(4 * TQ - SHARE, 4 * TQ)
            only = (lambda body: body) if layer == 0 else unless_local
            passes = NQ // (4 * LOADS)

            def slot(i, u, back=0):
                return i * LOADS + (LOADS + 1 + u - back)

            def pair(i, k, back=0):
                return i * (2 * LOADS) + (2 * LOADS + 1 + k - back)

            def group(i, q, back=0):
                return i * (4 * LOADS) + (4 * LOADS + 1 + q - back)

            def later(body, i, u):
                body(i + u // LOADS, u % LOADS)

            with nc.Block() as block:
                @block.sync
                @only
                def _(e):
                    r = sorted_rows.rearrange("(c q p t) w -> c p q (t w)", q=4, p=P, t=TQ)
                    with e.Fori(0, passes) as i:
                        for u in range(LOADS):
                            e.wait_ge(oh, pair(i, 2 * u + 1, 2 * LOADS))
                            e.dma_start(q_rows[u].rearrange("p q t w -> p q (t w)"),
                                        r[bass.ds(i * LOADS + u, 1), :, :, :].rearrange("c p q n -> (c p) q n")
                                        ).then_inc(ld[u], 16)
                    for u in range(LOADS):
                        e.wait_ge(ld[u], 16 * passes)

                @block.scalar
                @only
                def _(e):
                    seed(e, p1, p2, ev, n=LOADS)

                    def first_part(i, u):
                        e.wait_ge(ld[u], i * 16 + 16)
                        e.wait_ge(mm, pair(i, 2 * u + 1, 2 * LOADS))
                        e.copy(parts[u][0], data[u]).then_inc(p1, 1)

                    def second_part(i, u):
                        e.wait_ge(r1, slot(i, u))
                        e.wait_ge(r1_v, slot(i, u))
                        e.copy(parts[u][1], left[u]).then_inc(p2, 1)

                    def take_sums(i, u):
                        e.wait_ge(ac, group(i, 4 * u + 3, 8))
                        e.wait_ge(mm, pair(i, 2 * u + 1))
                        e.copy(sums[u % 2], slot_sums(u)).then_inc(ev, 1)

                    for u in range(3):
                        first_part(0, u)
                    second_part(0, 0)
                    with e.Fori(0, passes - 1) as i:
                        for u in range(LOADS):
                            later(second_part, i, u + 1)
                            take_sums(i, u)
                            later(first_part, i, u + 3)
                    for u in range(LOADS):
                        if u + 1 < LOADS:
                            second_part(passes - 1, u + 1)
                        take_sums(passes - 1, u)
                        if u + 3 < LOADS:
                            first_part(passes - 1, u + 3)

                @block.gpsimd
                @only
                def _(e):
                    seed(e, r1, n=LOADS)
                    seed(e, ac, n=4 * LOADS)

                    def first_part(i, u):
                        e.wait_ge(p3, slot(i, u, LOADS))
                        e.wait_ge(p1, slot(i, u))
                        e.tensor_tensor(left[u][:, pool_tiles, :], data[u][:, pool_tiles, :],
                                        parts[u][0][:, pool_tiles, :], ALU.subtract).then_inc(r1, 1)

                    def add(i, u):
                        _, blocks = nc.values_load_multi_w_load_instructions(
                            q_row[0:1, bass.ds(i * (4 * LOADS) + u * 4, 4)], engines=[mybir.EngineType.Pool],
                            min_val=0, max_val=NB)
                        e.wait_ge(ev, slot(i, u))
                        for q, b in enumerate(blocks):
                            e.wait_ge(ac, group(i, 4 * u + q, 1))
                            to = agg[:, bass.ds(b, 1), :].rearrange("p b d -> p (b d)")
                            e.tensor_tensor(to, to, sums[u % 2][:, q, :], ALU.add).then_inc(ac, 1)

                    first_part(0, 0)
                    first_part(0, 1)
                    with e.Fori(0, passes - 1) as i:
                        for u in range(LOADS):
                            later(first_part, i, u + 2)
                            add(i, u)
                    for u in range(LOADS):
                        if u + 2 < LOADS:
                            first_part(passes - 1, u + 2)
                        add(passes - 1, u)

                @block.tensor
                @only
                def _(e):
                    seed(e, mm, n=2 * LOADS)
                    with e.Fori(0, passes) as i:
                        for u in range(LOADS):
                            e.wait_ge(p3, slot(i, u))
                            e.wait_ge(ev, slot(i, u, 2))
                            for k in range(2):
                                e.wait_ge(oh, pair(i, 2 * u + k))
                                for n in range(2 * TQ):
                                    q, t = 2 * k + n // TQ, n % TQ
                                    for c in range(PARTS):
                                        last = e.matmul(slot_sums(u)[:, q, :], q_onehot[k][:, n, :],
                                                        parts[u][c][:, q * TQ + t, :],
                                                        start=(t == 0 and c == 0),
                                                        stop=(t == TQ - 1 and c == PARTS - 1))
                                last.then_inc(mm, 1)

                @block.vector
                @only
                def _(e):
                    seed(e, oh, n=2 * LOADS)
                    seed(e, p3, r1_v, n=LOADS)

                    def first_part(i, u):
                        e.wait_ge(p3, slot(i, u, LOADS))
                        e.wait_ge(p1, slot(i, u))
                        e.tensor_tensor(left[u][:, vector_tiles, :], data[u][:, vector_tiles, :],
                                        parts[u][0][:, vector_tiles, :], ALU.subtract).then_inc(r1_v, 1)

                    def rows_onehot(i, u, k):
                        e.wait_ge(mm, pair(i, 2 * u + k, 2))
                        place = q_rows[u][:, 2 * k:2 * k + 2, :, D:D + 1]
                        e.tensor_tensor(q_onehot[k],
                                        place.rearrange("p q t w -> p (q t) w").broadcast_to([P, 2 * TQ, P]),
                                        iota[:, None, 0:P].broadcast_to([P, 2 * TQ, P]), ALU.is_equal).then_inc(oh, 1)

                    def sums_of(i, u, ahead):
                        e.wait_ge(ld[u], i * 16 + 16)
                        rows_onehot(i, u, 0)
                        e.wait_ge(p2, slot(i, u))
                        e.tensor_tensor(parts[u][2], left[u], parts[u][1], ALU.subtract).then_inc(p3, 1)
                        if ahead:
                            later(first_part, i, u + 1)
                        rows_onehot(i, u, 1)

                    first_part(0, 0)
                    with e.Fori(0, passes - 1) as i:
                        for u in range(LOADS):
                            sums_of(i, u, True)
                    for u in range(LOADS):
                        sums_of(passes - 1, u, u + 1 < LOADS)

        def center(e, step, at):
            a, n = agg[:, at, :], at.stop - at.start
            mean = stat[0][:, at]
            step(e.tensor_reduce(mean, a, AX.X, ALU.add))
            step(e.tensor_scalar(mean, mean, 1.0 / D, None, ALU.mult))
            return e.tensor_tensor(a, a, mean.unsqueeze(2).broadcast_to([P, n, D]), ALU.subtract)

        def sum_squares(e, at):
            return e.tensor_reduce(stat[0][:, at], tmp[:, at, :], AX.X, ALU.add)

        def root(e, at):
            return e.activation(stat[1][:, at], stat[0][:, at], ACT.Sqrt, scale=1.0 / D, bias=eps[:, 0:1])

        def scale(e, step, to, at):
            step(e.reciprocal(stat[0][:, at], stat[1][:, at]))
            by = stat[0][:, at].unsqueeze(2).broadcast_to([P, at.stop - at.start, D])
            return e.tensor_tensor(to[:, at, :], agg[:, at, :], by, ALU.mult)

        def square(e, at):
            return e.activation(tmp[:, at, :], agg[:, at, :], ACT.Square)

        def in_turn(n, *stages):
            for now in range(n + len(stages) - 1):
                for k, stage in enumerate(stages):
                    if 0 <= now - k < n:
                        stage(now - k)

        def node_update():
            d_, g_, cen, sq, var, rt, nrm, gam, cen2, sq2, var2, rt2, nrm2, cp, o_ = (sem(f"n0_{k}") for k in (
                "d", "g", "cen", "sq", "var", "rt", "nrm", "gam", "cen2", "sq2", "var2", "rt2", "nrm2", "cp", "o"))
            size = -(-NB // 7)
            chunks = [slice(b, min(b + size, NB)) for b in range(0, NB, size)]
            n = len(chunks)
            bc = lambda a, at: a[:, None, :].broadcast_to([P, at.stop - at.start, D])
            with nc.Block() as block:
                @block.vector
                def _(e):
                    step = stepper(e, d_)
                    step(e.memset(x1[:, NB:NBP, :], 0.0))
                    e.memset(agg[:, NB:NBP, :], 0.0)

                    def first_center(c):
                        center(e, step, chunks[c]).then_inc(cen, 1)

                    def first_sum(c):
                        e.wait_ge(sq, c + 1)
                        sum_squares(e, chunks[c]).then_inc(var, 1)

                    def first_scale(c):
                        e.wait_ge(rt, c + 1)
                        scale(e, step, agg, chunks[c]).then_inc(nrm, 1)

                    def second_center(c):
                        e.wait_ge(gam, c + 1)
                        center(e, step, chunks[c]).then_inc(cen2, 1)

                    def second_sum(c):
                        e.wait_ge(sq2, c + 1)
                        sum_squares(e, chunks[c]).then_inc(var2, 1)

                    def second_scale(c):
                        e.wait_ge(rt2, c + 1)
                        scale(e, step, x1, chunks[c]).then_inc(nrm2, 1)
                    in_turn(n, first_center, first_sum, first_scale, lambda c: None,
                            second_center, second_sum, second_scale)

                @block.scalar
                def _(e):
                    def first_square(c):
                        e.wait_ge(cen, c + 1)
                        square(e, chunks[c]).then_inc(sq, 1)

                    def first_root(c):
                        e.wait_ge(var, c + 1)
                        root(e, chunks[c]).then_inc(rt, 1)

                    def second_square(c):
                        e.wait_ge(cen2, c + 1)
                        square(e, chunks[c]).then_inc(sq2, 1)

                    def second_root(c):
                        e.wait_ge(var2, c + 1)
                        root(e, chunks[c]).then_inc(rt2, 1)

                    def copy(c):
                        e.wait_ge(nrm2, c + 1)
                        e.copy(agg[:, chunks[c], :], x1[:, chunks[c], :]).then_inc(cp, 1)
                    in_turn(n, first_square, first_root, lambda c: None, lambda c: None,
                            second_square, second_root, copy)

                @block.gpsimd
                def _(e):
                    step = stepper(e, g_)
                    for c, at in enumerate(chunks):
                        a, x_ = agg[:, at, :], xs[:, at, :]
                        step(e.tensor_tensor(x_, x_, bc(wts["beta"], at), ALU.add))
                        e.wait_ge(nrm, c + 1)
                        step(e.tensor_tensor(a, a, bc(wts["gamma"], at), ALU.mult))
                        e.tensor_tensor(a, a, x_, ALU.add).then_inc(gam, 1)

                @block.sync
                def _(e):
                    r = x1_rows.rearrange("(b p) d -> p b d", p=P)
                    for c, at in enumerate(chunks):
                        e.wait_ge(nrm2, c + 1)
                        e.dma_start(r[:, at, :], x1[:, at, :]).then_inc(o_, 16)
                    e.wait_ge(o_, 16 * n)

        def refill():
            f_, z_ = sem("refill"), sem("refill_zeros")
            zero_rows = tmp_space[:, 0:FR * W]
            with nc.Block() as block:
                @block.gpsimd
                @unless_local
                def _(e):
                    e.memset(zero_rows, 0.0).then_inc(z_, 1)

                @block.sync
                @unless_local
                def _(e):
                    e.wait_ge(z_, 1)
                    with e.Fori(0, FILL) as c:
                        e.dma_start(fill[bass.ds(c, 1), :, :].rearrange("c p n -> (c p) n"), zero_rows).then_inc(f_, 16)
                    e.wait_ge(f_, 16 * FILL)

                @block.vector
                def _(e):
                    for s in shared.values():
                        e.sem_clear(s)

        def node_mlp():
            d_, t_, ev, h1, re, f2, f1, b_, cen, sq, var, rt, nrm, o_ = (sem(f"n1_{k}") for k in (
                "d", "t", "ev", "h1", "re", "f2", "f1", "b", "cen", "sq", "var", "rt", "nrm", "o"))
            G = NBP // T
            blocks = [slice(g * T, (g + 1) * T) for g in range(G)]
            real = [slice(g * T, min((g + 1) * T, NB)) for g in range(G)]
            with nc.Block() as block:
                @block.gpsimd
                def _(e):
                    for g in range(G):
                        e.tensor_tensor(x1[:, blocks[g], :], x1[:, blocks[g], :],
                                        wts["b2"][:, None, :].broadcast_to([P, T, D]), ALU.add).then_inc(b_, 1)

                @block.vector
                def _(e):
                    step = stepper(e, d_)

                    def add_and_center(g):
                        e.wait_ge(f2, g + 1)
                        e.wait_ge(b_, g + 1)
                        step(e.tensor_tensor(agg[:, blocks[g], :], ps_f[:, :].rearrange("p (t d) -> p t d", d=D),
                                             x1[:, blocks[g], :], ALU.add))
                        e.sem_inc(f1, 1)
                        center(e, step, real[g]).then_inc(cen, 1)

                    def sum_(g):
                        e.wait_ge(sq, g + 1)
                        sum_squares(e, real[g]).then_inc(var, 1)

                    def scale_(g):
                        e.wait_ge(rt, g + 1)
                        scale(e, step, agg, real[g]).then_inc(nrm, 1)
                    in_turn(G, add_and_center, sum_, scale_)

                @block.tensor
                def _(e):
                    def transposes(g):
                        e.wait_ge(ev, g)
                        for k in range(T // 2):
                            pair = agg[:, g * T + 2 * k:g * T + 2 * k + 2, :].rearrange("p b d -> p (b d)")
                            last = e.transpose(ps_t[:, k * P:(k + 1) * P], pair, ident[:, :])
                        last.then_inc(t_, 1)

                    def products(g):
                        e.wait_ge(re, g)
                        e.wait_ge(ev, g + 1)
                        e.matmul(ps_h[:, :], wts["w1"][:, :], in_t[:, :], start=True, stop=True).then_inc(h1, 1)
                        if g + 1 < G:
                            transposes(g + 1)
                        e.wait_ge(f1, g)
                        e.wait_ge(re, g + 1)
                        for k in range(T // 2):
                            last = e.matmul(ps_f[:, k * P:(k + 1) * P], hid_t[:, k * P:(k + 1) * P],
                                            wts["w2"][:, :], start=True, stop=True)
                        last.then_inc(f2, 1)
                    transposes(0)
                    for g in range(G):
                        products(g)

                @block.scalar
                def _(e):
                    def hidden(g):
                        e.wait_ge(h1, g)
                        e.wait_ge(t_, g + 1)
                        e.activation(in_t[:, :], ps_t[:, :], ACT.Copy).then_inc(ev, 1)
                        e.wait_ge(f2, g)
                        e.wait_ge(h1, g + 1)
                        e.activation(hid_t[:, :], ps_h[:, :], ACT.Relu, bias=wts["b1"][:, 0:1]).then_inc(re, 1)

                    def square_(g):
                        e.wait_ge(cen, g + 1)
                        square(e, real[g]).then_inc(sq, 1)

                    def root_(g):
                        e.wait_ge(var, g + 1)
                        root(e, real[g]).then_inc(rt, 1)
                    in_turn(G, hidden, square_, root_)

                @block.sync
                def _(e):
                    r = out.rearrange("(b p) d -> p b d", p=P)
                    for g in range(G):
                        e.wait_ge(nrm, g + 1)
                        e.dma_start(r[:, real[g], :], agg[:, real[g], :]).then_inc(o_, 16)
                    e.wait_ge(o_, 16 * G)

        s_pad = sem("s_pad")
        s_go = sem("s_go")
        set_up(counting(0, hi_s))
        messages(0, hi_s, lo_s, dst_i, wxh_rows)
        reduce_rows(0)
        node_update()
        window_sums()
        refill()
        count_again(1, hi_d)
        messages(1, hi_d, lo_d, src_i, x1_rows)
        reduce_rows(1)
        node_mlp()


def kernel(x, src, dst, edge_attr_64, edge_weight, L0_gnn_Wf1, L0_gnn_bf1, L0_gnn_Wf2, L0_gnn_bf2, L0_gnn_Wl,
           L0_gnn_bl, L0_gnn_gamma, L0_gnn_beta, L1_gnn_W1, L1_gnn_b1, L1_gnn_W2, L1_gnn_b2):
    import concourse.bacc as bacc
    import numpy as np
    from concourse.bass_utils import run_bass_kernel_spmd

    x, src, dst, rbf, ew = (np.asarray(a) for a in (x, src, dst, edge_attr_64, edge_weight))
    n_nodes, n_edges = x.shape[0], src.shape[0]
    NB, NBP, NG, NQ = sizes(n_nodes, n_edges)
    pad_node = (2 * NB) * P

    def edges(a, fill):
        a = np.concatenate([a, np.full(NG * T * P - n_edges, fill, a.dtype)])
        return np.ascontiguousarray(a.reshape(NG, P, T).transpose(1, 0, 2).reshape(P, NG * T))

    def twice(a):
        a = np.asarray(a)
        z = np.zeros_like(a)
        return np.ascontiguousarray(np.block([[a, z], [z, a]]))

    def column(a):
        return np.ascontiguousarray(np.concatenate([a, a]).reshape(P, 1))

    def spread(a):
        return np.ascontiguousarray(np.broadcast_to(np.asarray(a), (P, D)))

    w = {
        "wf1": twice(np.asarray(L0_gnn_Wf1).T), "wf2": twice(np.asarray(L0_gnn_Wf2).T),
        "wl": twice(np.asarray(L0_gnn_Wl).T), "w1": twice(L1_gnn_W1), "w2": twice(L1_gnn_W2),
        "bf1": column(L0_gnn_bf1), "b1": column(L1_gnn_b1),
        "bf2": spread(L0_gnn_bf2), "bl": spread(L0_gnn_bl), "gamma": spread(L0_gnn_gamma),
        "beta": spread(L0_gnn_beta), "b2": spread(L1_gnn_b2),
    }
    arrays = {
        "x": np.concatenate([x, np.zeros((NBP * P - n_nodes, D), x.dtype)]),
        "src": edges(src, pad_node), "dst": edges(dst, pad_node), "ew": edges(ew, 0),
        "rbf": np.concatenate([rbf, np.zeros((NG * T * P - n_edges, D), rbf.dtype)]),
        **{f"w_{k}_dram": a for k, a in w.items()},
    }
    nc = bacc.Bacc("TRN2", target_bir_lowering=False, num_devices=1)
    ap = {k: nc.dram_tensor(k, a.shape, mybir.dt.from_np(a.dtype), kind="ExternalInput").ap()
          for k, a in arrays.items()}
    out = nc.dram_tensor("out", (NB * P, D), F32, kind="ExternalOutput").ap()
    wxh_rows = nc.dram_tensor("wxh_rows", (NBP * P, D), F32).ap()
    x1_rows = nc.dram_tensor("x1_rows", (NB * P, D), F32).ap()
    sorted_rows = nc.dram_tensor("sorted_rows", (NQ * ROWS_Q, W), F32).ap()
    q_block_row = nc.dram_tensor("q_block_row", (1, -(-NQ // P) * P), I32).ap()
    seed_rows = nc.dram_tensor("seed_rows", (S, 16), BF16).ap()
    rel_rows = nc.dram_tensor("rel_rows", (-(-NG * T // P) * P, P), BF16).ap()
    program(nc, n_nodes, n_edges, ap["x"], ap["src"], ap["dst"], ap["ew"], ap["rbf"],
            {k: ap[f"w_{k}_dram"] for k in w}, out, wxh_rows, x1_rows, sorted_rows, q_block_row, seed_rows, rel_rows)
    r = run_bass_kernel_spmd(nc, [arrays], core_ids=[0])
    return r.results[0]["out"][:n_nodes]
```
